# Optimizing a Trainium2 kernel written in Bass

```python
import numpy as np
import jax
import jax.numpy as jnp

def _softmax(x, axis=-1):
    return jax.nn.softmax(x, axis=axis)

def _gelu(x):
    return jax.nn.gelu(x, approximate=True)

def _silu(x):
    return jax.nn.silu(x)

def _sigmoid(x):
    return jax.nn.sigmoid(x)

def _layernorm(x, axis=-1, eps=1e-05):
    m = jnp.mean(x, axis=axis, keepdims=True)
    v = jnp.var(x, axis=axis, keepdims=True)
    return (x - m) / jnp.sqrt(v + eps)

def _scatter_add(tgt, idx, src, axis=0):
    return tgt.at[idx].add(src)

def _segment_sum(src, seg, n):
    return jax.ops.segment_sum(src, seg, n)
kernel_name = 'mk_flamingo_gated_d1_seqx_r2_133ca2'

def setup_inputs(seed: int=0):
    np.random.seed(seed)
    _w = jnp.asarray

    def _rec_inputs():
        import jax
        import jax.numpy as jnp
        _rk = jax.random.key(seed)
        x = -0.0002928 + 1 * jax.random.normal(jax.random.fold_in(_rk, 1), (16, 512, 512), jnp.float32)
        _lenS = 512 - jax.random.randint(jax.random.fold_in(_rk, 7), (16,), 0, max(1, 512 // 4) + 1, jnp.int32)
        _lenS2 = 512 - jax.random.randint(jax.random.fold_in(_rk, 8), (16,), 0, max(1, 512 // 4) + 1, jnp.int32)
        _ctx_1024P = jax.random.normal(jax.random.fold_in(_rk, 11), (16, 16, 512), jnp.float32)
        _ctx_1024c = jax.random.dirichlet(jax.random.fold_in(_rk, 511), 0.3 * jnp.ones((16,), jnp.float32), (16, 512))
        _ctx_1024t = jnp.einsum('bsk,bkd->bsd', _ctx_1024c, _ctx_1024P)
        _ctx_1024t = _ctx_1024t * jax.lax.rsqrt(jnp.mean(jnp.square(_ctx_1024t)) + 1e-12) * 0.953939
        ctx_1024 = -1.39393e-06 + 0.999914 * (_ctx_1024t + 0.3 * jax.random.normal(jax.random.fold_in(_rk, 611), (16, 512, 512), jnp.float32))
        _validS = jnp.arange(512)[None, :] < _lenS[:, None]
        _validS2 = jnp.arange(512)[None, :] < _lenS2[:, None]
        _causal = jnp.tril(jnp.ones((512, 512), dtype=bool))
        mask_SxS2_bk0 = jnp.logical_not(jnp.broadcast_to(_validS2[0:1, :], (512, 512)))
        _g = jax.random.normal(jax.random.fold_in(_rk, 9001), (2, 1), jnp.float32)
        _g = jnp.sign(_g) * jnp.maximum(jnp.abs(_g), 1.0) + (_g == 0) * 1.0
        g_xattn = _g[0]
        g_ffn = _g[1]
        return (x, ctx_1024, mask_SxS2_bk0, g_xattn, g_ffn)
    x, ctx_1024, mask_SxS2_bk0, g_xattn, g_ffn = _rec_inputs()

    def _L0_xattn_setup():
        import jax, jax.numpy as jnp
        import numpy as np
        B, S, IN_DIM = (2, 1024, 512)
        DIMS, QH, KVH = (512, 16, 4)
        HD = DIMS // QH
        G = QH // KVH
        key = jax.random.key(seed)
        k1, k2, k3, k4, k5, k6 = jax.random.split(key, 6)
        scale = 0.02
        q_in = jax.random.normal(k1, (B, S, IN_DIM), dtype=jnp.float32)
        kv_in = jax.random.normal(k2, (B, S, IN_DIM), dtype=jnp.float32)
        mask = jnp.tril(jnp.ones((S, S), dtype=bool))
        Wq = jax.random.normal(k3, (IN_DIM, QH, HD), dtype=jnp.float32) * scale
        Wk = jax.random.normal(k4, (IN_DIM, KVH, HD), dtype=jnp.float32) * scale
        Wv = jax.random.normal(k5, (IN_DIM, KVH, HD), dtype=jnp.float32) * scale
        Wo = jax.random.normal(k6, (KVH * HD, IN_DIM), dtype=jnp.float32) * scale
        return {'q_in': q_in, 'kv_in': kv_in, 'mask': mask, 'Wq': Wq, 'Wk': Wk, 'Wv': Wv, 'Wo': Wo}
    _L0_xattn_all = _L0_xattn_setup()
    _L0_xattn_in = {k: v for k, v in _L0_xattn_all.items() if k in ('Wq', 'Wk', 'Wv', 'Wo')}
    del _L0_xattn_all

    def _L0_ffn_setup():
        import jax, jax.numpy as jnp
        import numpy as np
        D_MODEL = 512
        FF = 2048
        E = 8
        TOP_K = 2
        CAP_FACTOR = 1.25
        B, T = (4, 1024)

        def _moe_forward(x, gate_w, gate_b, w1, b1, w2, b2):
            Bb, Tt, d = x.shape
            S = Bb * Tt
            C = int(CAP_FACTOR * S / E)
            xf = x.reshape(S, d)
            logits = xf @ gate_w + gate_b
            probs = jax.nn.softmax(logits, axis=1)
            topk_p, topk_i = jax.lax.top_k(probs, TOP_K)
            topk_pn = topk_p / jnp.sum(topk_p, axis=1, keepdims=True)
            rows = jnp.arange(S)
            w_te = jnp.zeros((S, E), xf.dtype).at[rows[:, None], topk_i].set(topk_pn)
            mask = jnp.zeros((S, E), bool).at[rows[:, None], topk_i].set(True)
            rank = jnp.cumsum(mask.astype(jnp.int32), axis=0)
            slot = jnp.where(mask & (rank <= C), rank - 1, C)
            e_grid = jnp.broadcast_to(jnp.arange(E), (S, E))
            t_grid = jnp.broadcast_to(rows[:, None], (S, E))
            buf = jnp.full((E, C + 1), S, jnp.int32).at[e_grid, slot].set(t_grid)
            idx = buf[:, :C]
            valid = idx < S
            x_pad = jnp.concatenate([xf, jnp.zeros((1, d), xf.dtype)], axis=0)
            xin = x_pad[idx]
            h = jax.nn.relu(jnp.einsum('ecd,edh->ech', xin, w1) + b1[:, None, :])
            out = jnp.einsum('ech,ehd->ecd', h, w2) + b2[:, None, :]
            w_pad = jnp.concatenate([w_te, jnp.zeros((1, E), xf.dtype)], axis=0)
            tok_w = w_pad[idx, jnp.arange(E)[:, None]]
            out = out * jnp.where(valid, tok_w, 0.0)[:, :, None]
            final = jnp.zeros((S + 1, d), xf.dtype).at[idx.reshape(-1)].add(out.reshape(-1, d))[:S]
            return final.reshape(Bb, Tt, d)
        key = jax.random.key(seed)
        ks = jax.random.split(key, 7)
        s = 0.02
        return {'x': jax.random.normal(ks[0], (B, T, D_MODEL), jnp.float32), 'gate_w': jax.random.normal(ks[1], (D_MODEL, E), jnp.float32) * s, 'gate_b': jnp.zeros((E,), jnp.float32), 'w1': jax.random.normal(ks[2], (E, D_MODEL, FF), jnp.float32) * s, 'b1': jnp.zeros((E, FF), jnp.float32), 'w2': jax.random.normal(ks[3], (E, FF, D_MODEL), jnp.float32) * s, 'b2': jnp.zeros((E, D_MODEL), jnp.float32)}
    _L0_ffn_all = _L0_ffn_setup()
    _L0_ffn_in = {k: v for k, v in _L0_ffn_all.items() if k in ('gate_w', 'gate_b', 'w1', 'b1', 'w2', 'b2')}
    del _L0_ffn_all
    return {'x': x, 'ctx_1024': ctx_1024, 'mask_SxS2_bk0': mask_SxS2_bk0, 'g_xattn': g_xattn, 'g_ffn': g_ffn, 'L0_xattn_Wq': _L0_xattn_in['Wq'], 'L0_xattn_Wk': _L0_xattn_in['Wk'], 'L0_xattn_Wv': _L0_xattn_in['Wv'], 'L0_xattn_Wo': _L0_xattn_in['Wo'], 'L0_ffn_gate_w': _L0_ffn_in['gate_w'], 'L0_ffn_gate_b': _L0_ffn_in['gate_b'], 'L0_ffn_w1': _L0_ffn_in['w1'], 'L0_ffn_b1': _L0_ffn_in['b1'], 'L0_ffn_w2': _L0_ffn_in['w2'], 'L0_ffn_b2': _L0_ffn_in['b2']}

def reference(x, ctx_1024, mask_SxS2_bk0, g_xattn, g_ffn, L0_xattn_Wq, L0_xattn_Wk, L0_xattn_Wv, L0_xattn_Wo, L0_ffn_gate_w, L0_ffn_gate_b, L0_ffn_w1, L0_ffn_b1, L0_ffn_w2, L0_ffn_b2):
    import jax
    import jax.numpy as jnp

    def _L0_xattn_ref(q_in, kv_in, mask, Wq, Wk, Wv, Wo):
        import jax, jax.numpy as jnp
        import numpy as np
        B, S, IN_DIM = (2, 1024, 512)
        DIMS, QH, KVH = (512, 16, 4)
        HD = DIMS // QH
        G = QH // KVH
        b, s, _ = q_in.shape
        q = jnp.einsum('bsi,ihd->bshd', q_in, Wq)
        k = jnp.einsum('bsi,ihd->bshd', kv_in, Wk)
        v = jnp.einsum('bsi,ihd->bshd', kv_in, Wv)
        q_g = q.reshape(b, s, KVH, G, HD).sum(axis=3)
        q_g = jnp.transpose(q_g, (0, 2, 1, 3))
        k = jnp.transpose(k, (0, 2, 1, 3))
        v = jnp.transpose(v, (0, 2, 1, 3))
        scores = jnp.einsum('bhsd,bhad->bhsa', q_g, k)
        scores = jnp.where(mask[None, None, :, :], scores, -jnp.inf)
        attn = jax.nn.softmax(scores / HD ** 0.5, axis=-1)
        out = jnp.einsum('bhsa,bhad->bhsd', attn, v)
        out = jnp.transpose(out, (0, 2, 1, 3)).reshape(b, s, KVH * HD)
        return out @ Wo

    def _L0_ffn_ref(x, gate_w, gate_b, w1, b1, w2, b2):
        import jax, jax.numpy as jnp
        import numpy as np
        D_MODEL = 512
        FF = 2048
        E = 8
        TOP_K = 2
        CAP_FACTOR = 1.25
        B, T = (4, 1024)

        def _moe_forward(x, gate_w, gate_b, w1, b1, w2, b2):
            Bb, Tt, d = x.shape
            S = Bb * Tt
            C = int(CAP_FACTOR * S / E)
            xf = x.reshape(S, d)
            logits = xf @ gate_w + gate_b
            probs = jax.nn.softmax(logits, axis=1)
            topk_p, topk_i = jax.lax.top_k(probs, TOP_K)
            topk_pn = topk_p / jnp.sum(topk_p, axis=1, keepdims=True)
            rows = jnp.arange(S)
            w_te = jnp.zeros((S, E), xf.dtype).at[rows[:, None], topk_i].set(topk_pn)
            mask = jnp.zeros((S, E), bool).at[rows[:, None], topk_i].set(True)
            rank = jnp.cumsum(mask.astype(jnp.int32), axis=0)
            slot = jnp.where(mask & (rank <= C), rank - 1, C)
            e_grid = jnp.broadcast_to(jnp.arange(E), (S, E))
            t_grid = jnp.broadcast_to(rows[:, None], (S, E))
            buf = jnp.full((E, C + 1), S, jnp.int32).at[e_grid, slot].set(t_grid)
            idx = buf[:, :C]
            valid = idx < S
            x_pad = jnp.concatenate([xf, jnp.zeros((1, d), xf.dtype)], axis=0)
            xin = x_pad[idx]
            h = jax.nn.relu(jnp.einsum('ecd,edh->ech', xin, w1) + b1[:, None, :])
            out = jnp.einsum('ech,ehd->ecd', h, w2) + b2[:, None, :]
            w_pad = jnp.concatenate([w_te, jnp.zeros((1, E), xf.dtype)], axis=0)
            tok_w = w_pad[idx, jnp.arange(E)[:, None]]
            out = out * jnp.where(valid, tok_w, 0.0)[:, :, None]
            final = jnp.zeros((S + 1, d), xf.dtype).at[idx.reshape(-1)].add(out.reshape(-1, d))[:S]
            return final.reshape(Bb, Tt, d)
        return _moe_forward(x, gate_w, gate_b, w1, b1, w2, b2)
    x = x + jnp.tanh(g_xattn[0]) * _L0_xattn_ref(_layernorm(x, axis=-1), ctx_1024, mask_SxS2_bk0, L0_xattn_Wq, L0_xattn_Wk, L0_xattn_Wv, L0_xattn_Wo)
    x = x + jnp.tanh(g_ffn[0]) * _L0_ffn_ref(_layernorm(x, axis=-1), L0_ffn_gate_w, L0_ffn_gate_b, L0_ffn_w1, L0_ffn_b1, L0_ffn_w2, L0_ffn_b2)
    return x

_drawn_inputs = setup_inputs


def setup_inputs(seed=0):
    import zlib

    import numpy as np

    out = dict(_drawn_inputs(seed))
    spreads = {'L0_ffn_gate_b': (0.0, 0.1), 'L0_ffn_b1': (0.0, 0.1), 'L0_ffn_b2': (0.0, 0.1)}
    factors = {'L0_xattn_Wq': 4.13, 'L0_xattn_Wk': 3.99}
    for name, (base, spread) in spreads.items():
        noise = np.random.default_rng([zlib.crc32(name.encode()), seed]).standard_normal(out[name].shape)
        drawn = base * np.exp(spread * noise) if base else spread * noise
        out[name] = jnp.asarray(drawn.astype(out[name].dtype))
    for name, factor in factors.items():
        out[name] = (out[name] * factor).astype(out[name].dtype)
    return out
```

```python
from contextlib import ExitStack

import numpy as np

import concourse.bass as bass
from concourse import mybir

ALU = mybir.AluOpType
ACT = mybir.ActivationFunctionType
AX = mybir.AxisListType
F32 = mybir.dt.float32
F32R = mybir.dt.float32r
I32 = mybir.dt.int32
U32 = mybir.dt.uint32
U8 = mybir.dt.uint8

P = 128
BATCHES, S, D = 16, 512, 512
TOKENS = BATCHES * S
NT = S // P
ND = D // P
QH, KVH, HD = 16, 4, 32
G = QH // KVH
PARTS = P // HD
UNITS = NT * KVH
E, TOP_K, FF = 8, 2, 2048
NF = FF // P
CAP = int(1.25 * TOKENS / E)
CT = CAP // P
ROWS = TOKENS + CAP
EPS = 1e-5
SCALE = float(HD) ** -0.5
MASKED = -3.0e38
FAR = 65536.0


def since(eng, sem, count, passed=None):
    if isinstance(count, int):
        if count > 0:
            eng.wait_ge(sem, count)
    else:
        eng.wait_ge(sem, count)
        if passed is not None:
            eng.sem_inc(passed, 1)


def product(nc, out, w_hi, w_lo, x_hi, x_lo, start, stop):
    nc.tensor.matmul(out, w_lo, x_hi, start=start, stop=False)
    nc.tensor.matmul(out, w_hi, x_lo, start=False, stop=False)
    return nc.tensor.matmul(out, w_hi, x_hi, start=False, stop=stop)


def attention_phase(nc, a):
    with ExitStack() as ctx:
        def sb(name, shape, dt=F32):
            return ctx.enter_context(nc.sbuf_tensor(name, shape, dt))

        def ps(name, shape):
            return ctx.enter_context(nc.psum_tensor(name, shape, F32))

        def sem(name):
            return ctx.enter_context(nc.semaphore(name))

        ident = sb("ident", [P, P])
        upto = sb("upto", [P, P])
        ones = sb("ones", [P, P])
        zeros = sb("zeros", [P, D])
        minus_half = sb("minus_half", [P, NT])
        expert_no = sb("expert_no", [P, E])
        slot_base = sb("slot_base", [P, E])
        unused = sb("unused", [P, E * CT, 2], I32)
        mask_u8 = sb("mask_u8", [P, NT, S], U8)
        mask_bias = sb("mask_bias", [P, NT, S])
        wk_raw = sb("wk_raw", [P, ND, P])
        wv_raw = sb("wv_raw", [P, ND, P])
        wo_raw = sb("wo_raw", [P, D])
        w_split = {n: (sb(f"w{n}_hi", [P, ND, P], F32R), sb(f"w{n}_lo", [P, ND, P], F32R)) for n in "qkv"}
        wq_sum = sb("wq_sum", [P, ND, P])
        wo_hi, wo_lo = sb("wo_hi", [P, D], F32R), sb("wo_lo", [P, D], F32R)
        gate_w = sb("gate_w", [P, ND, E])
        gate_b = sb("gate_b", [P, E])
        g_raw = sb("g_raw", [P, 2])
        g_tanh = sb("g_tanh", [P, 2])

        x_sb = sb("x_sb", [P, NT, D])
        ctx_sb = sb("ctx_sb", [P, NT, D])
        xn = sb("xn", [P, NT, D])
        xT = (sb("xT_hi", [P, ND, S], F32R), sb("xT_lo", [P, ND, S], F32R))
        cT = (sb("cT_hi", [P, ND, S], F32R), sb("cT_lo", [P, ND, S], F32R))
        k_flat = (sb("k_hi", [P, S], F32R), sb("k_lo", [P, S], F32R))
        q_flat = (sb("q_hi", [P, S], F32R), sb("q_lo", [P, S], F32R))
        k_stack = [sb(f"k_stack{i}", [P, KVH, S], F32R) for i in range(2)]
        q_stack = [sb(f"q_stack{i}", [P, KVH, S], F32R) for i in range(2)]
        v_sb = [sb(f"v{i}", [P, NT, P]) for i in range(2)]
        stats = sb("stats", [P, NT, 6])
        mean_var = sb("mean_var", [P, NT, 2])
        rstd = sb("rstd", [P, NT])
        shift = sb("shift", [P, NT])
        probs = sb("probs", [P, 4, S])
        row_min = sb("row_min", [P, 4, 1])
        row_sum = sb("row_sum", [P, UNITS])
        pT_sb = sb("pT_sb", [P, 2, S])
        inv_sum = sb("inv_sum", [P, KVH])
        o_sb = sb("o_sb", [P, P])
        oT_hi, oT_lo = sb("oT_hi", [P, P], F32R), sb("oT_lo", [P, P], F32R)
        x_again = sb("x_again", [P, 2, D])
        x2 = sb("x2", [P, 2, D])
        stats2 = sb("stats2", [P, 6])
        mean_var2 = sb("mean_var2", [P, 2])
        rstd2 = sb("rstd2", [P, 1])
        shift2 = sb("shift2", [P, 1])
        xn2 = sb("xn2", [P, 2, D])
        xn2T = sb("xn2T", [P, ND, P])
        logits = sb("logits", [P, NT, E])
        best = sb("best", [P, NT, 8])
        best_no = sb("best_no", [P, NT, 8], U32)
        best_f = sb("best_f", [P, NT, TOP_K])
        chosen = sb("chosen", [P, TOP_K, NT, E])
        either = sb("either", [P, NT, E])
        before = sb("before", [P, E])
        prior = sb("prior", [P, NT, E])
        gap = sb("gap", [P, NT])
        ratio = sb("ratio", [P, NT])
        denom = sb("denom", [P, NT])
        share = sb("share", [P, NT])
        slot_e = sb("slot_e", [P, NT, E])
        over_e = sb("over_e", [P, NT, E])
        picked = sb("picked", [P, TOP_K, NT, E])
        slot_f = sb("slot_f", [P, TOP_K, NT])
        slot_i = sb("slot_i", [P, TOP_K, NT], I32)
        token_f = sb("token_f", [P, NT])
        info = sb("info", [P, TOP_K, NT, 2], I32)

        score_ps = ps("score_ps", [P, 2, S])
        pT_ps = ps("pT_ps", [P, 2, S])
        a_ps = ps("a_ps", [P, 2, S])
        y_ps = ps("y_ps", [P, S])
        o_bank = ps("o_bank", [P, S])
        o_ps, oT_ps, logit_ps = o_bank[:, 0:P], y_ps[:, 0:P], y_ps[:, 0:E]

        passed = sem("passed")
        weights_in = sem("weights_in")
        consts_set = sem("consts_set")
        tanh_set = sem("tanh_set")
        prepared = sem("prepared")
        prep_step = sem("prep_step")
        tables_set = sem("tables_set")
        x_in = sem("x_in")
        ctx_in = sem("ctx_in")
        k_stacked = sem("k_stacked")
        q_stacked = sem("q_stacked")
        again_in = [sem(f"again_in{i}") for i in range(2)]
        x2_out = [sem(f"x2_out{i}") for i in range(2)]
        xn2_out = [sem(f"xn2_out{i}") for i in range(2)]
        routed = sem("routed")
        stats_set = sem("stats_set")
        aggr_set = sem("aggr_set")
        ln_step = sem("ln_step")
        xn_set = sem("xn_set")
        a_made = sem("a_made")
        a_hi = sem("a_hi")
        a_lo = sem("a_lo")
        scored = sem("scored")
        masked = sem("masked")
        exped = sem("exped")
        turned = sem("turned")
        pT_even = sem("pT_even")
        pT_odd = sem("pT_odd")
        weighed = sem("weighed")
        inv_set = sem("inv_set")
        o_set = sem("o_set")
        oT_made = sem("oT_made")
        oT_hi_set = sem("oT_hi_set")
        oT_lo_set = sem("oT_lo_set")
        y_made = sem("y_made")
        x2_set = sem("x2_set")
        stats2_set = sem("stats2_set")
        aggr2_set = sem("aggr2_set")
        ln2_step = sem("ln2_step")
        xn2_set = sem("xn2_set")
        xn2T_made = sem("xn2T_made")
        xn2T_set = sem("xn2T_set")
        logits_made = sem("logits_made")
        logits_set = sem("logits_set")
        gate_step = sem("gate_step")
        gate_pool = sem("gate_pool")
        ratio_set = sem("ratio_set")
        ranked = sem("ranked")
        before_step = sem("before_step")
        info_step = sem("info_step")

        A_STEPS = [("c", 0), ("c", 1), ("c", 2), ("c", 3), ("k", 0), ("v", 0),
                   ("x", 0), ("x", 1), ("x", 2), ("x", 3), ("q", 0)]
        NA = len(A_STEPS)
        LO_AT = {j: n for n, j in enumerate(j for j, (what, _) in enumerate(A_STEPS) if what != "v")}
        NLO = len(LO_AT)
        J_K, J_V, J_Q = 4, 5, 10
        LOADS = 9
        NCONST = 13
        NTABLES = 2 * (ROWS - TOKENS) // P + 1
        GD, GP = 11, 5
        RING = [("A", 0), ("A", 1), ("X", 1), ("A", 2), ("A", 3), ("A", 4), ("A", 5), ("X", 2), ("A", 6),
                ("A", 7), ("A", 8), ("A", 9), ("X", 3), ("A", 10), ("X", 0), ("R", 0)]
        assert len(RING) % 2 == 0

        def ring_bank(user):
            return a_ps[:, RING.index(user) % 2]

        def ring_free(eng, user, b):
            r = RING.index(user)
            while True:
                r -= 2
                what, k = RING[r % len(RING)]
                of = b + r // len(RING)
                if isinstance(of, int) and of < -1:
                    return
                seq = {"A": of + 1, "X": of if k == 0 else of - 1, "R": of - 1}[what]
                if not isinstance(seq, int) or 0 <= seq < BATCHES:
                    break
            if what == "A":
                since(eng, a_hi, seq * NA + k + 1)
                since(eng, a_lo, seq * NLO + sum(j <= k for j in LO_AT))
            elif what == "X":
                since(eng, xn2T_set, seq * NT + k + 1)
            else:
                since(eng, gate_step, (seq + 1) * GD + 7)

        x_v = a["x"].rearrange("b (t p) d -> b p t d", p=P)
        c_v = a["ctx"].rearrange("b (t p) d -> b p t d", p=P)
        x_t = a["x"].rearrange("b (t p) d -> (b t) p d", p=P)
        out_t = a["out"].rearrange("(n p) d -> n p d", p=P)
        tab_t = a["xn2_table"].rearrange("(n p) d -> n p d", p=P)

        def bodies(emit, eng):
            emit(-1, 1, False, False, True)
            emit(0, 0, True, False, True)
            with eng.Fori(0, (BATCHES - 4) // 2) as i:
                emit(i * 2 + 1, 1, True, True, True)
                emit(i * 2 + 2, 0, True, True, True)
            emit(BATCHES - 3, 1, True, True, True)
            emit(BATCHES - 2, 0, True, True, True)
            emit(BATCHES - 1, 1, True, True, False)
            emit(BATCHES, 0, False, True, False)

        def due(slot, b, par, main, prev, n, first, every=1):
            for at, bb, pp, live in ((slot, b, par, main), (slot + UNITS, b - 1, 1 - par, prev)):
                k, rest = divmod(at - first, every)
                if live and rest == 0 and 0 <= k < n:
                    return k, bb, pp
            return None

        block = ctx.enter_context(nc.Block())

        @block.sync
        def _(sp):
            sp.dma_start(x_sb[:], x_v[0]).then_inc(x_in, 16)
            sp.dma_start(ctx_sb[:], c_v[0]).then_inc(ctx_in, 16)
            loads = [(wk_raw[:], a["wk"].rearrange("(c p) h e -> p c (h e)", p=P)),
                     (wv_raw[:], a["wv"].rearrange("(c p) h e -> p c (h e)", p=P)),
                     (xn[:], a["wq"].rearrange("(c p) h e -> p c (h e)", p=P)),
                     (mask_u8[:], a["mask"].rearrange("(t p) k -> p t k", p=P)),
                     (wo_raw[:], a["wo"]),
                     (gate_w[:], a["gate_w"].rearrange("(c p) e -> p c e", p=P)),
                     (gate_b[:], a["gate_b"].partition_broadcast(P)),
                     (g_raw[:, 0:1], a["g_xattn"].partition_broadcast(P)),
                     (g_raw[:, 1:2], a["g_ffn"].partition_broadcast(P))]
            assert len(loads) == LOADS
            for to, of in loads:
                sp.dma_start(to, of).then_inc(weights_in, 16)
            sp.wait_ge(consts_set, NCONST)
            for n in range(TOKENS // P, ROWS // P):
                sp.dma_start(out_t[n], zeros[:]).then_inc(tables_set, 16)
                sp.dma_start(tab_t[n], zeros[:]).then_inc(tables_set, 16)
            sp.dma_start(a["slot_table"].rearrange("(n p) c -> p n c", p=P), unused[:]).then_inc(tables_set, 16)
            sp.wait_ge(tables_set, 16 * NTABLES)

            def emit(b, par, main, prev, nxt):
                n = b + 1
                for s in range(UNITS):
                    if s == 5 and nxt and not (isinstance(n, int) and n == BATCHES - 1):
                        since(sp, a_made, n * NA + 4, passed)
                        sp.dma_start(ctx_sb[:], c_v[n + 1]).then_inc(ctx_in, 16)
                    if s == 6 and nxt and not (isinstance(n, int) and n == BATCHES - 1):
                        since(sp, xn_set, n * NT + NT, passed)
                        sp.dma_start(x_sb[:], x_v[n + 1]).then_inc(x_in, 16)
                    if s == 6 and nxt:
                        stack(n, 1 - par, k_stack, k_flat, (0, 1, 0, 1), J_K, k_stacked)
                    if s == 11 and nxt:
                        stack(n, 1 - par, q_stack, q_flat, (0, 0, 1, 1), J_Q, q_stacked)
                    if it := due(s, b, par, main, prev, NT, 5, 4):
                        q, bb, _ = it
                        since(sp, x2_set, bb * NT + q - 1, passed)
                        sp.dma_start(x_again[:, q % 2], x_t[bb * NT + q]).then_inc(again_in[q % 2], 16)
                    if it := due(s, b, par, main, prev, NT, 11, 4):
                        q, bb, _ = it
                        since(sp, x2_set, bb * NT + q + 1, passed)
                        sp.dma_start(out_t[bb * NT + q], x2[:, q % 2]).then_inc(x2_out[q % 2], 16)
                    if it := due(s, b, par, main, prev, NT, 13, 4):
                        q, bb, _ = it
                        since(sp, xn2_set, bb * NT + q + 1, passed)
                        sp.dma_start(tab_t[bb * NT + q], xn2[:, q % 2]).then_inc(xn2_out[q % 2], 16)

            def stack(n, par, to, of, parts, j, done):
                since(sp, a_hi, n * NA + j + 1, passed)
                since(sp, a_lo, n * NLO + LO_AT[j] + 1, passed)
                for g, part in enumerate(parts):
                    for h in range(KVH):
                        sp.dma_start(to[par][g * HD:(g + 1) * HD, h, :].bitcast(F32),
                                     of[part][h * HD:(h + 1) * HD, :].bitcast(F32)).then_inc(done, 16)

            bodies(emit, sp)
            for i in range(2):
                sp.wait_ge(x2_out[i], 16 * BATCHES * NT // 2)
                sp.wait_ge(xn2_out[i], 16 * BATCHES * NT // 2)

        @block.gpsimd
        def _(pool):
            nc.gpsimd.memset(ident[:], 0.0).then_inc(consts_set, 1)
            nc.gpsimd.memset(upto[:], 1.0).then_inc(consts_set, 1)
            nc.gpsimd.memset(ones[:], 1.0).then_inc(consts_set, 1)
            nc.gpsimd.memset(zeros[:], 0.0).then_inc(consts_set, 1)
            nc.gpsimd.memset(minus_half[:], -0.5).then_inc(consts_set, 1)
            nc.gpsimd.memset(unused[:], 0).then_inc(consts_set, 1)
            nc.gpsimd.memset(before[:], 0.0).then_inc(consts_set, 1)
            nc.gpsimd.iota(expert_no[:], [[1, E]], base=0, channel_multiplier=0,
                           allow_small_or_imprecise_dtypes=True).then_inc(consts_set, 1)
            nc.gpsimd.iota(slot_base[:], [[CAP, E]], base=-1, channel_multiplier=0,
                           allow_small_or_imprecise_dtypes=True).then_inc(consts_set, 1)
            nc.gpsimd.iota(token_f[:], [[P, NT]], base=0, channel_multiplier=1,
                           allow_small_or_imprecise_dtypes=True).then_inc(consts_set, 1)
            pool.wait_ge(consts_set, 10)
            nc.gpsimd.affine_select(out=ident[:], in_=ident[:], compare_op=ALU.not_equal, fill=1.0, base=0,
                                    pattern=[[-1, P]], channel_multiplier=1).then_inc(consts_set, 1)
            nc.gpsimd.affine_select(out=upto[:], in_=upto[:], compare_op=ALU.is_ge, fill=0.0, base=0,
                                    pattern=[[1, P]], channel_multiplier=-1).then_inc(consts_set, 1)
            nc.gpsimd.iota(unused[:, :, 0].rearrange("p (e t) -> p e t", e=E), [[0, E], [P, CT]], base=TOKENS,
                           channel_multiplier=1).then_inc(consts_set, 1)
            pool.wait_ge(tables_set, 16 * NTABLES)
            pool.wait_ge(tanh_set, 1)

            def layernorm_scale(r, sh, mean, var, half, chain, done):
                nc.gpsimd.tensor_scalar(r, var, EPS, None, ALU.add).then_inc(chain, 1)
                nc.gpsimd.tensor_scalar(sh, mean, -1.0, None, ALU.mult).then_inc(chain, 1)
                since(pool, chain, done + 2, passed)
                nc.gpsimd.tensor_tensor(r, r, half, ALU.pow).then_inc(chain, 1)
                since(pool, chain, done + 3, passed)
                nc.gpsimd.tensor_tensor(sh, sh, r, ALU.mult).then_inc(chain, 1)
                since(pool, chain, done + 4, passed)

            def emit(b, par, main, prev, nxt):
                n = b + 1
                for s in range(UNITS):
                    if s == 4 and nxt:
                        since(pool, aggr_set, n * NT + NT, passed)
                        since(pool, xn_set, n * NT, passed)
                        layernorm_scale(rstd[:], shift[:], mean_var[:, :, 0], mean_var[:, :, 1],
                                        minus_half[:], ln_step, n * 4)
                        since(pool, a_made, (n - 1) * NA + J_Q, passed)
                        if isinstance(n, int) and n == 0:
                            pool.wait_ge(prepared, 1)
                        for t in range(NT):
                            nc.gpsimd.tensor_scalar(xn[:, t], x_sb[:, t], rstd[:, t:t + 1], shift[:, t:t + 1],
                                                    ALU.mult, ALU.add).then_inc(xn_set, 1)
                    if it := due(s, b, par, main, prev, NT, 11, 4):
                        q, bb, _ = it
                        m = bb * NT + q
                        since(pool, aggr2_set, m + 1, passed)
                        since(pool, xn2_set, m, passed)
                        layernorm_scale(rstd2[:], shift2[:], mean_var2[:, 0:1], mean_var2[:, 1:2],
                                        minus_half[:, 0:1], ln2_step, m * 4)
                        since(pool, xn2_out[q % 2], (bb * 2 + q // 2) * 16, passed)
                        since(pool, xn2T_made, m - 1, passed)
                        nc.gpsimd.tensor_scalar(xn2[:, q % 2], x2[:, q % 2], rstd2[:], shift2[:],
                                                ALU.mult, ALU.add).then_inc(xn2_set, 1)
                    if it := due(s, b, par, main, prev, 1, 28):
                        _, bb, _ = it
                        since(pool, gate_step, (bb + 1) * GD + 4, passed)
                        nc.gpsimd.tensor_tensor(either[:], chosen[:, 0], chosen[:, 1], ALU.add).then_inc(gate_pool, 1)
                        nc.gpsimd.tensor_copy(prior[:, 0], before[:]).then_inc(gate_pool, 1)
                        nc.gpsimd.tensor_tensor(gap[:], best[:, :, 1], best[:, :, 0], ALU.subtract)\
                            .then_inc(gate_pool, 1)
                        since(pool, gate_pool, bb * GP + 3, passed)
                        for t in range(NT):
                            nc.gpsimd.tensor_tensor(prior[:, t + 1] if t < NT - 1 else before[:], prior[:, t],
                                                    either[:, t], ALU.add)\
                                .then_inc(before_step, 1)
                            since(pool, before_step, bb * NT + t + 1, passed)
                    if it := due(s, b, par, main, prev, 1, 30):
                        _, bb, _ = it
                        since(pool, gate_step, (bb + 1) * GD + 6, passed)
                        for k in range(TOP_K):
                            nc.gpsimd.tensor_copy(info[:, k, :, 0], token_f[:]).then_inc(info_step, 1)
                        nc.gpsimd.tensor_scalar(info[:, 0, :, 1].bitcast(F32), share[:], g_tanh[:, 1:2], None,
                                                ALU.mult).then_inc(info_step, 1)
                        nc.gpsimd.tensor_tensor(ratio[:], ratio[:], share[:], ALU.mult).then_inc(gate_pool, 1)
                        since(pool, gate_pool, bb * GP + 4, passed)
                        nc.gpsimd.tensor_scalar(info[:, 1, :, 1].bitcast(F32), ratio[:], g_tanh[:, 1:2], None,
                                                ALU.mult).then_inc(info_step, 1)
                        since(pool, info_step, bb * 4 + 4, passed)
                        nc.gpsimd.tensor_scalar(token_f[:], token_f[:], float(S), None, ALU.add).then_inc(gate_pool, 1)
                    if it := due(s, b, par, main, prev, 1, 31):
                        _, bb, _ = it
                        since(pool, gate_step, (bb + 1) * GD + GD, passed)
                        for k in range(TOP_K):
                            for t in range(NT):
                                nc.gpsimd.indirect_dma_start(
                                    out=a["slot_table"], out_offset=bass.IndirectOffsetOnAxis(
                                        ap=slot_i[:, k, t:t + 1], axis=0),
                                    in_=info[:, k, t, :], in_offset=None,
                                    bounds_check=E * CAP - 1, oob_is_err=False).then_inc(routed, 16)
                        since(pool, routed, (bb + 1) * (TOP_K * NT * 16), passed)

            bodies(emit, pool)

        @block.scalar
        def _(act):
            act.wait_ge(weights_in, 16 * LOADS)
            nc.scalar.activation(g_tanh[:], g_raw[:], ACT.Tanh).then_inc(tanh_set, 1)

            def emit(b, par, main, prev, nxt):
                n = b + 1
                for s in range(UNITS):
                    if it := due(s, b, par, main, prev, UNITS, 1):
                        u, bb, _ = it
                        act.wait_ge(masked, bb * UNITS + u + 1)
                        nc.scalar.activation(probs[:, u % 4], probs[:, u % 4], ACT.Exp, bias=row_min[:, u % 4],
                                             scale=-1.0, accum_out=row_sum[:, u:u + 1]).then_inc(exped, 1)
                    if nxt and s < NA:
                        what, k = A_STEPS[s]
                        bank = ring_bank(("A", s))
                        act.wait_ge(a_made, n * NA + s + 1)
                        if what in "cx":
                            since(act, a_made, (n - 1) * NA + (J_V if what == "c" else J_Q) + 1)
                            to = (cT if what == "c" else xT)[0][:, k]
                        elif what == "v":
                            to = v_sb[1 - par][:].rearrange("p t e -> p (t e)")
                        else:
                            since(act, k_stacked if what == "k" else q_stacked, n * (PARTS * KVH * 16))
                            to = (k_flat if what == "k" else q_flat)[0][:]
                        nc.scalar.activation(to, bank, ACT.Copy).then_inc(a_hi, 1)
                    if it := due(s, b, par, main, prev, NT, 8, 4):
                        q, bb, _ = it
                        act.wait_ge(oT_made, bb * NT + q + 1)
                        since(act, y_made, bb * NT + q)
                        nc.scalar.activation(oT_hi[:], oT_ps, ACT.Copy).then_inc(oT_hi_set, 1)
                    if it := due(s, b, par, main, prev, NT, 13, 4):
                        q, bb, pp = it
                        act.wait_ge(xn2T_made, bb * NT + q + 1)
                        since(act, logits_made, bb * NT + q)
                        nc.scalar.activation(xn2T[:].rearrange("p c t -> p (c t)"), ring_bank(("X", q)), ACT.Copy)\
                            .then_inc(xn2T_set, 1)
                    if (it := due(s, b, par, main, prev, UNITS, 2)) and it[0] % 2 == 1:
                        u, bb, _ = it
                        act.wait_ge(turned, bb * UNITS + u + 1)
                        since(act, weighed, bb * UNITS + u - 1)
                        nc.scalar.activation(pT_sb[:, 1], pT_ps[:, 1], ACT.Copy).then_inc(pT_odd, 1)
                    if it := due(s, b, par, main, prev, 1, 29):
                        _, bb, _ = it
                        act.wait_ge(gate_pool, bb * GP + 3)
                        nc.scalar.activation(ratio[:], gap[:], ACT.Exp).then_inc(ratio_set, 1)

            bodies(emit, act)

        @block.vector
        def _(dve):
            prep = [0]

            def then(ins):
                prep[0] += 1
                ins.then_inc(prep_step, 1)
                dve.wait_ge(prep_step, prep[0])

            dve.wait_ge(weights_in, 16 * LOADS)
            for c in range(ND):
                last = nc.vector.tensor_reduce(
                    wq_sum[:, c].rearrange("p (h e) -> p h e", h=KVH),
                    xn[:, c].rearrange("p (h g e) -> p h e g", h=KVH, g=G), AX.X, ALU.add)
            then(last)
            dve.wait_ge(tanh_set, 1)
            then(nc.vector.tensor_scalar(wo_raw[:], wo_raw[:], g_tanh[:, 0:1], None, ALU.mult))
            splits = [(wq_sum[:], *w_split["q"]), (wk_raw[:], *w_split["k"]), (wv_raw[:], *w_split["v"]),
                      (wo_raw[:], wo_hi, wo_lo)]
            for raw, hi, lo in splits:
                last = nc.vector.tensor_copy(hi[:], raw)
            then(last)
            for raw, hi, lo in splits:
                last = nc.vector.tensor_tensor(lo[:], raw, hi[:].bitcast(F32), ALU.subtract)
            last.then_inc(gate_step, GD)
            nc.vector.tensor_scalar(mask_bias[:], mask_u8[:], 1.0, -MASKED, ALU.subtract, ALU.mult)\
                .then_inc(prepared, 1)
            dve.wait_ge(prepared, 1)
            dve.wait_ge(consts_set, NCONST)

            def emit(b, par, main, prev, nxt):
                n = b + 1
                for s in range(UNITS):
                    if it := due(s, b, par, main, prev, NT, 7, 4):
                        q, bb, _ = it
                        m = bb * NT + q
                        dve.wait_ge(weighed, bb * UNITS + 4 * q + 4)
                        since(dve, oT_made, m)
                        nc.vector.reciprocal(inv_sum[:], row_sum[:, 4 * q:4 * q + 4]).then_inc(inv_set, 1)
                        dve.wait_ge(inv_set, m + 1)
                        nc.vector.tensor_tensor(
                            o_sb[:].rearrange("p (h e) -> p h e", h=KVH),
                            o_ps.rearrange("p (h e) -> p h e", h=KVH),
                            inv_sum[:].unsqueeze(2).to_broadcast([P, KVH, HD]), ALU.mult).then_inc(o_set, 1)
                    if it := due(s, b, par, main, prev, NT, 10, 4):
                        q, bb, _ = it
                        m = bb * NT + q
                        dve.wait_ge(y_made, m + 1)
                        dve.wait_ge(again_in[q % 2], (bb * 2 + q // 2 + 1) * 16)
                        since(dve, x2_out[q % 2], (bb * 2 + q // 2) * 16)
                        since(dve, xn2_set, m - 1)
                        nc.vector.tensor_tensor(x2[:, q % 2], y_ps[:], x_again[:, q % 2], ALU.add).then_inc(x2_set, 1)
                    if main:
                        q, h = divmod(s, KVH)
                        since(dve, scored, b * UNITS + s + 1, passed)
                        since(dve, turned, b * UNITS + s - 3, passed)
                        nc.vector.tensor_tensor_reduce(probs[:, s % 4], score_ps[:, s % 2], mask_bias[:, q], -SCALE,
                                                       1e30, ALU.add, ALU.min, row_min[:, s % 4]).then_inc(masked, 1)
                    if nxt and s in LO_AT:
                        what, k = A_STEPS[s]
                        hi, lo = {"c": cT, "x": xT, "k": k_flat, "q": q_flat}[what]
                        if what in "cx":
                            hi, lo = hi[:, k], lo[:, k]
                        else:
                            hi, lo = hi[:], lo[:]
                        dve.wait_ge(a_hi, n * NA + s + 1)
                        nc.vector.tensor_tensor(lo, ring_bank(("A", s)), hi.bitcast(F32), ALU.subtract)\
                            .then_inc(a_lo, 1)
                    if it := due(s, b, par, main, prev, NT, 8, 4):
                        q, bb, _ = it
                        dve.wait_ge(oT_hi_set, bb * NT + q + 1)
                        nc.vector.tensor_tensor(oT_lo[:], oT_ps, oT_hi[:].bitcast(F32), ALU.subtract)\
                            .then_inc(oT_lo_set, 1)
                    if nxt and 1 <= s <= NT:
                        since(dve, stats_set, n * NT + s, passed)
                        since(dve, ln_step, n * 4, passed)
                        nc.vector.bn_aggr(mean_var[:, s - 1], stats[:, s - 1]).then_inc(aggr_set, 1)
                    if it := due(s, b, par, main, prev, NT, 10, 4):
                        q, bb, _ = it
                        dve.wait_ge(x2_set, bb * NT + q + 1)
                        nc.vector.bn_stats(stats2[:], x2[:, q % 2]).then_inc(stats2_set, 1)
                    if (it := due(s, b, par, main, prev, UNITS, 2)) and it[0] % 2 == 0:
                        u, bb, _ = it
                        dve.wait_ge(turned, bb * UNITS + u + 1)
                        since(dve, weighed, bb * UNITS + u - 1)
                        nc.vector.tensor_copy(pT_sb[:, 0], pT_ps[:, 0]).then_inc(pT_even, 1)
                    if it := due(s, b, par, main, prev, NT, 15, 4):
                        q, bb, _ = it
                        dve.wait_ge(logits_made, bb * NT + q + 1)
                        nc.vector.tensor_tensor(logits[:, q], logit_ps, gate_b[:], ALU.add).then_inc(logits_set, 1)
                    if it := due(s, b, par, main, prev, NT, 10, 4):
                        q, bb, _ = it
                        m = bb * NT + q
                        since(dve, stats2_set, m + 1, passed)
                        since(dve, ln2_step, m * 4, passed)
                        nc.vector.bn_aggr(mean_var2[:], stats2[:]).then_inc(aggr2_set, 1)
                    if nxt and s < NT:
                        dve.wait_ge(x_in, (n + 1) * 16)
                        nc.vector.bn_stats(stats[:, s], x_sb[:, s]).then_inc(stats_set, 1)
                    if it := due(s, b, par, main, prev, 1, 27):
                        _, bb, _ = it
                        g = (bb + 1) * GD
                        since(dve, logits_set, (bb + 1) * NT, passed)
                        for t in range(NT):
                            last = nc.vector.max(best[:, t], logits[:, t])
                        last.then_inc(gate_step, 1)
                        since(dve, gate_step, g + 1, passed)
                        for t in range(NT):
                            last = nc.vector.max_index(best_no[:, t], best[:, t], logits[:, t])
                        last.then_inc(gate_step, 1)
                        dve.wait_ge(gate_step, g + 2)
                        nc.vector.tensor_copy(best_f[:], best_no[:, :, 0:TOP_K]).then_inc(gate_step, 1)
                        dve.wait_ge(gate_step, g + 3)
                        for k in range(TOP_K):
                            last = nc.vector.tensor_tensor(
                                chosen[:, k], expert_no[:].unsqueeze(1).to_broadcast([P, NT, E]),
                                best_f[:, :, k:k + 1].to_broadcast([P, NT, E]), ALU.is_equal)
                        last.then_inc(gate_step, 1)
                    if it := due(s, b, par, main, prev, 1, 30):
                        _, bb, _ = it
                        g = (bb + 1) * GD
                        dve.wait_ge(ratio_set, bb + 1)
                        nc.vector.tensor_scalar(denom[:], ratio[:], 1.0, None, ALU.add).then_inc(gate_step, 1)
                        dve.wait_ge(gate_step, g + 5)
                        nc.vector.reciprocal(share[:], denom[:]).then_inc(gate_step, 1)
                    if it := due(s, b, par, main, prev, 1, 31):
                        _, bb, _ = it
                        g = (bb + 1) * GD
                        dve.wait_ge(ranked, bb + 1)
                        ranks = ring_bank(("R", 0))[:, 0:NT * E].rearrange("p (t e) -> p t e", e=E)
                        nc.vector.tensor_tensor(slot_e[:], ranks, slot_base[:].unsqueeze(1).to_broadcast([P, NT, E]),
                                                ALU.add)
                        nc.vector.tensor_scalar(over_e[:], ranks, float(CAP), FAR, ALU.is_gt, ALU.mult)\
                            .then_inc(gate_step, 1)
                        dve.wait_ge(gate_step, g + 7)
                        nc.vector.tensor_tensor(slot_e[:], slot_e[:], over_e[:], ALU.add).then_inc(gate_step, 1)
                        dve.wait_ge(gate_step, g + 8)
                        for k in range(TOP_K):
                            last = nc.vector.tensor_tensor(picked[:, k], chosen[:, k], slot_e[:], ALU.mult)
                        last.then_inc(gate_step, 1)
                        dve.wait_ge(gate_step, g + 9)
                        nc.vector.tensor_reduce(slot_f[:], picked[:], AX.X, ALU.add).then_inc(gate_step, 1)
                        dve.wait_ge(gate_step, g + 10)
                        nc.vector.tensor_copy(slot_i[:], slot_f[:]).then_inc(gate_step, 1)

            bodies(emit, dve)

        @block.tensor
        def _(pe):
            pe.wait_ge(prepared, 1)
            pe.wait_ge(consts_set, NCONST)

            def turn(to, of):
                return nc.tensor.transpose(to, of, ident[:])

            def prepare(n, par, j):
                what, k = A_STEPS[j]
                bank = ring_bank(("A", j))
                ring_free(pe, ("A", j), n - 1)
                if what in "cx":
                    if what == "c":
                        pe.wait_ge(ctx_in, (n + 1) * 16)
                    else:
                        pe.wait_ge(xn_set, (n + 1) * NT)
                    of = ctx_sb if what == "c" else xn
                    for t in range(NT):
                        last = turn(bank[:, t * P:(t + 1) * P], of[:, t, k * P:(k + 1) * P])
                else:
                    through = 4 if what in "kv" else 10
                    pe.wait_ge(a_hi, n * NA + through)
                    pe.wait_ge(a_lo, n * NLO + sum(i < through for i in LO_AT))
                    w_hi, w_lo = w_split[what]
                    x_hi, x_lo = xT if what == "q" else cT
                    if what == "v":
                        for t in range(NT):
                            for c in range(ND):
                                last = product(nc, bank[:, t * P:(t + 1) * P], x_hi[:, c, t * P:(t + 1) * P],
                                               x_lo[:, c, t * P:(t + 1) * P], w_hi[:, c], w_lo[:, c],
                                               c == 0, c == ND - 1)
                    else:
                        for c in range(ND):
                            last = product(nc, bank, w_hi[:, c], w_lo[:, c], x_hi[:, c], x_lo[:, c],
                                           c == 0, c == ND - 1)
                last.then_inc(a_made, 1)

            def emit(b, par, main, prev, nxt):
                n = b + 1
                for s in range(UNITS):
                    if main:
                        q, h = divmod(s, KVH)
                        if s == 0:
                            pe.wait_ge(k_stacked, (b + 1) * (PARTS * KVH * 16))
                            pe.wait_ge(q_stacked, (b + 1) * (PARTS * KVH * 16))
                        since(pe, masked, b * UNITS + s - 1)
                        nc.tensor.matmul(score_ps[:, s % 2], q_stack[par][:, h, q * P:(q + 1) * P], k_stack[par][:, h],
                                         start=True, stop=True).then_inc(scored, 1)
                    if nxt and s < NA:
                        prepare(n, 1 - par, s)
                    if it := due(s, b, par, main, prev, UNITS, 2):
                        u, bb, _ = it
                        pe.wait_ge(exped, bb * UNITS + u + 1)
                        since(pe, pT_odd if u % 2 else pT_even, bb * (UNITS // 2) + u // 2)
                        for t in range(NT):
                            last = turn(pT_ps[:, u % 2, t * P:(t + 1) * P], probs[:, u % 4, t * P:(t + 1) * P])
                        last.then_inc(turned, 1)
                    if it := due(s, b, par, main, prev, NT, 8, 4):
                        q, bb, _ = it
                        m = bb * NT + q
                        pe.wait_ge(o_set, m + 1)
                        since(pe, x2_set, m)
                        since(pe, logits_set, m - 1)
                        turn(oT_ps, o_sb[:]).then_inc(oT_made, 1)
                    if it := due(s, b, par, main, prev, NT, 9, 4):
                        q, bb, _ = it
                        m = bb * NT + q
                        pe.wait_ge(oT_hi_set, m + 1)
                        pe.wait_ge(oT_lo_set, m + 1)
                        product(nc, y_ps[:], oT_hi[:], oT_lo[:], wo_hi[:], wo_lo[:], True, True).then_inc(y_made, 1)
                    if it := due(s, b, par, main, prev, NT, 13, 4):
                        q, bb, pp = it
                        bank = ring_bank(("X", q))
                        pe.wait_ge(xn2_set, bb * NT + q + 1)
                        ring_free(pe, ("X", q), b)
                        for c in range(ND):
                            last = turn(bank[:, c * P:(c + 1) * P], xn2[:, q % 2, c * P:(c + 1) * P])
                        last.then_inc(xn2T_made, 1)
                    if it := due(s, b, par, main, prev, NT, 15, 4):
                        q, bb, _ = it
                        pe.wait_ge(xn2T_set, bb * NT + q + 1)
                        since(pe, logits_set, bb * NT + q)
                        y_count = bb * NT + q + 2
                        pe.wait_ge(x2_set, min(y_count, BATCHES * NT) if isinstance(y_count, int) else y_count)
                        for c in range(ND):
                            last = nc.tensor.matmul(logit_ps, xn2T[:, c], gate_w[:, c],
                                                    start=(c == 0), stop=(c == ND - 1))
                        last.then_inc(logits_made, 1)
                    if it := due(s, b, par, main, prev, 1, 31):
                        _, bb, _ = it
                        pe.wait_ge(before_step, bb * NT + NT)
                        ring_free(pe, ("R", 0), b)
                        to = ring_bank(("R", 0))[:, 0:NT * E]
                        nc.tensor.matmul(to, upto[:], either[:].rearrange("p t e -> p (t e)"), start=True, stop=False)
                        nc.tensor.matmul(to, ones[:], prior[:].rearrange("p t e -> p (t e)"), start=False, stop=True)\
                            .then_inc(ranked, 1)
                    if it := due(s, b, par, main, prev, UNITS, 3):
                        u, bb, pp = it
                        q, h = divmod(u, KVH)
                        pe.wait_ge(pT_odd if u % 2 else pT_even, bb * (UNITS // 2) + u // 2 + 1)
                        if u == 0:
                            pe.wait_ge(a_hi, bb * NA + J_V + 1)
                        if h == 0:
                            since(pe, o_set, bb * NT + q)
                        for t in range(NT):
                            last = nc.tensor.matmul(o_ps[:, h * HD:(h + 1) * HD], pT_sb[:, u % 2, t * P:(t + 1) * P],
                                                    v_sb[pp][:, t, h * HD:(h + 1) * HD],
                                                    start=(t == 0), stop=(t == NT - 1))
                        last.then_inc(weighed, 1)

            bodies(emit, pe)


def expert_phase(nc, a):
    with ExitStack() as ctx:
        def sb(name, shape, dt=F32):
            return ctx.enter_context(nc.sbuf_tensor(name, shape, dt))

        def ps(name, shape):
            return ctx.enter_context(nc.psum_tensor(name, shape, F32))

        def sem(name):
            return ctx.enter_context(nc.semaphore(name))

        BLOCKS = [(0, 4), (4, 7), (7, 10)]
        NB = len(BLOCKS)
        STEPS = NB * NF
        WIDE = max(t1 - t0 for t0, t1 in BLOCKS)

        ident = sb("ident2", [P, P])
        w_hi = sb("w_hi", [P, NF, 2 * D], F32R)
        w_lo = sb("w_lo", [P, NF, 2 * D], F32R)
        staged = sb("staged", [P, 2, 2 * D])
        x_rows = sb("x_rows", [P, 2, D])
        xT_hi = sb("xT2_hi", [P, CT, ND, P], F32R)
        xT_lo = sb("xT2_lo", [P, CT, ND, P], F32R)
        h = sb("h", [P, 2, WIDE * P])
        h_hi = sb("h_hi", [P, 2, WIDE * P], F32R)
        h_lo = sb("h_lo", [P, 2, WIDE * P], F32R)
        y_sb = sb("y_sb", [P, WIDE, D])
        b1_rows = sb("b1_rows", [P, P])
        b1T = sb("b1T", [P, E * NF])
        b2 = sb("b2", [P, D])
        take = sb("take", [P, CT, 2], I32)
        give = sb("give", [P, CT, 2], I32)

        h_ps = ps("h_ps", [P, 2, D])
        y_ps = ps("y2_ps", [P, WIDE, D])
        t_ps = ps("t_ps", [P, 2, D])

        passed = sem("passed2")
        ident_set = sem("ident2_set")
        b1_in = sem("b1_in")
        b1_turned = sem("b1_turned")
        b1_set = sem("b1_set")
        b2_in = sem("b2_in")
        take_in = sem("take_in")
        give_in = sem("give_in")
        staged_in = [sem(f"staged_in{i}") for i in range(2)]
        w_hi_set = sem("w_hi_set")
        w_lo_set = sem("w_lo_set")
        gathered = [sem(f"gathered{i}") for i in range(2)]
        x_turned = sem("x_turned")
        xT_hi_set = sem("xT2_hi_set")
        xT_lo_set = sem("xT2_lo_set")
        h_made = sem("h_made")
        h_set = sem("h_set")
        h_lo_set = sem("h_lo_set")
        stepped = sem("stepped")
        y_made = sem("y2_made")
        y_set = sem("y_set")
        y_weighed = sem("y_weighed")
        added = [sem(f"added{i}") for i in range(WIDE)]

        w1_v = a["w1"].rearrange("e (c p) (f m) -> e f p c m", p=P, m=P)
        w2_v = a["w2"].rearrange("e (f p) d -> e f p d", p=P)
        slots_v = a["slot_table"].rearrange("(e t p) c -> e p t c", p=P, t=CT)

        def block_of(t):
            return next(i for i, (t0, t1) in enumerate(BLOCKS) if t0 <= t < t1)

        TURNS = {4: (0, 7), 7: (0, 8), 10: (0, 9), 19: (1, 0), 22: (1, 1), 25: (1, 2), 28: (1, 3),
                 35: (1, 4), 38: (1, 5), 41: (1, 6)}
        EARLY = 7
        AHEAD = 3

        def turn_at(g, e, last):
            if g in TURNS:
                later, t = TURNS[g]
                if not (later and last):
                    return e + later, t
            return None

        def refills_at(g, e, first, last):
            if first and g + AHEAD < NF:
                return e, g + AHEAD
            if not first and g < 2:
                return e, NF - 2 + g
            if not last and g >= STEPS - NF + 2:
                return e + 1, g - (STEPS - NF + 2)
            return None

        def experts(emit, eng):
            emit(0, True, False)
            with eng.Fori(1, E - 1) as e:
                emit(e, False, False)
            emit(E - 1, False, True)

        def uses(i, e, blk):
            return e * sum(i < t1 - t0 for t0, t1 in BLOCKS) + sum(i < t1 - t0 for t0, t1 in BLOCKS[:blk])

        block = ctx.enter_context(nc.Block())

        @block.sync
        def _(sp):
            def stage(e, f):
                since(sp, w_lo_set, e * NF + f - 1, passed)
                sp.dma_start(staged[:, f % 2, 0:D].rearrange("p (c m) -> p c m", c=ND), w1_v[e, f])\
                    .then_inc(staged_in[f % 2], 16)
                sp.dma_start(staged[:, f % 2, D:2 * D], w2_v[e, f]).then_inc(staged_in[f % 2], 16)

            sp.dma_start(take[:], slots_v[0]).then_inc(take_in, 16)
            stage(0, 0)
            stage(0, 1)
            sp.dma_start(b1_rows[:], a["b1"].rearrange("e (f m) -> (e f) m", m=P)).then_inc(b1_in, 16)
            stage(0, 2)

            def emit(e, first, last):
                for g in range(STEPS):
                    if g == 3:
                        for i in range(WIDE):
                            since(sp, added[i], uses(i, e, 0) * 16, passed)
                        sp.dma_start(give[:], slots_v[e]).then_inc(give_in, 16)
                        since(sp, y_set, e * CT, passed)
                        sp.dma_start(b2[:], a["b2"][e].partition_broadcast(P)).then_inc(b2_in, 16)
                    if g == 6 and not last:
                        for i in range(2):
                            since(sp, gathered[i], (e + 1) * (CT // 2 * 16), passed)
                        sp.dma_start(take[:], slots_v[e + 1]).then_inc(take_in, 16)
                    if of := refills_at(g, e, first, last):
                        stage(*of)

            experts(emit, sp)
            for i in range(WIDE):
                sp.wait_ge(added[i], uses(i, E, 0) * 16)

        @block.gpsimd
        def _(pool):
            nc.gpsimd.memset(ident[:], 0.0).then_inc(ident_set, 1)
            pool.wait_ge(ident_set, 1)
            nc.gpsimd.affine_select(out=ident[:], in_=ident[:], compare_op=ALU.not_equal, fill=1.0, base=0,
                                    pattern=[[-1, P]], channel_multiplier=1).then_inc(ident_set, 1)

            def gather(e, t):
                since(pool, take_in, (e + 1) * 16, passed)
                since(pool, x_turned, e * CT + t - 1, passed)
                nc.gpsimd.indirect_dma_start(
                    out=x_rows[:, t % 2], out_offset=None, in_=a["xn2_table"],
                    in_offset=bass.IndirectOffsetOnAxis(ap=take[:, t, 0:1], axis=0)).then_inc(gathered[t % 2], 16)

            for t in range(EARLY + 2):
                gather(0, t)

            def emit(e, first, last):
                for g in range(STEPS):
                    if of := turn_at(g, e, last):
                        ee, t = of
                        if t + 2 < CT:
                            gather(ee, t + 2)
                        elif not last:
                            gather(ee + 1, t + 2 - CT)
                    if g % NF == 2 and (g > 2 or not first):
                        scatter_block(*((e, g // NF - 1) if g > 2 else (e - 1, NB - 1)))

            def scatter_block(e, blk):
                t0, t1 = BLOCKS[blk]
                since(pool, give_in, (e + 1) * 16, passed)
                if blk == 0:
                    for i in range(WIDE):
                        since(pool, added[i], uses(i, e, 0) * 16, passed)
                for i in range(t1 - t0):
                    since(pool, y_weighed, e * CT + t0 + i + 1, passed)
                    nc.gpsimd.indirect_dma_start(
                        out=a["out"], out_offset=bass.IndirectOffsetOnAxis(ap=give[:, t0 + i, 0:1], axis=0),
                        in_=y_sb[:, i], in_offset=None, compute_op=ALU.add).then_inc(added[i], 16)

            experts(emit, pool)
            scatter_block(E - 1, NB - 1)

        @block.scalar
        def _(act):
            act.wait_ge(b1_turned, 1)
            nc.scalar.activation(b1T[:], t_ps[:, 1, 0:P], ACT.Copy).then_inc(b1_set, 1)

            def x_high(e, t):
                act.wait_ge(x_turned, e * CT + t + 1)
                since(act, h_made, (e - 1) * STEPS + NF * (block_of(t) + 1))
                nc.scalar.activation(xT_hi[:, t].rearrange("p c t -> p (c t)"), t_ps[:, t % 2], ACT.Copy)\
                    .then_inc(xT_hi_set, 1)

            def w_high(e, f):
                act.wait_ge(staged_in[f % 2], (e * (NF // 2) + f // 2 + 1) * 32)
                since(act, stepped, (e - 1) * STEPS + (NB - 1) * NF + f + 1)
                nc.scalar.activation(w_hi[:, f], staged[:, f % 2], ACT.Copy).then_inc(w_hi_set, 1)

            def weigh_block(e, blk):
                t0, t1 = BLOCKS[blk]
                act.wait_ge(give_in, (e + 1) * 16)
                for i in range(t1 - t0):
                    act.wait_ge(y_set, e * CT + t0 + i + 1)
                    nc.scalar.activation(y_sb[:, i], y_sb[:, i], ACT.Copy,
                                         scale=give[:, t0 + i, 1:2].bitcast(F32)).then_inc(y_weighed, 1)

            for t in range(4):
                x_high(0, t)
            for f in range(AHEAD):
                w_high(0, f)
            for t in range(4, EARLY):
                x_high(0, t)

            def emit(e, first, last):
                for g in range(STEPS):
                    blk, f = divmod(g, NF)
                    n = (BLOCKS[blk][1] - BLOCKS[blk][0]) * P
                    since(act, h_made, e * STEPS + g + 1, passed)
                    since(act, stepped, e * STEPS + g - 1, passed)
                    bias = b1T[:, bass.ds(e * NF + f, 1)]
                    nc.scalar.activation(h[:, g % 2, 0:n], h_ps[:, g % 2, 0:n], ACT.Relu, bias=bias)
                    nc.scalar.activation(h_hi[:, g % 2, 0:n], h_ps[:, g % 2, 0:n], ACT.Relu, bias=bias)\
                        .then_inc(h_set, 1)
                    if of := turn_at(g, e, last):
                        x_high(*of)
                    if of := refills_at(g, e, first, last):
                        w_high(*of)
                    if f == 1 and (g > 1 or not first):
                        weigh_block(*((e, blk - 1) if blk else (e - 1, NB - 1)))

            experts(emit, act)
            weigh_block(E - 1, NB - 1)

        @block.vector
        def _(dve):
            def x_low(e, t):
                dve.wait_ge(xT_hi_set, e * CT + t + 1)
                nc.vector.tensor_tensor(xT_lo[:, t].rearrange("p c t -> p (c t)"), t_ps[:, t % 2],
                                        xT_hi[:, t].rearrange("p c t -> p (c t)").bitcast(F32), ALU.subtract)\
                    .then_inc(xT_lo_set, 1)

            def w_low(e, f):
                dve.wait_ge(w_hi_set, e * NF + f + 1)
                nc.vector.tensor_tensor(w_lo[:, f], staged[:, f % 2], w_hi[:, f].bitcast(F32), ALU.subtract)\
                    .then_inc(w_lo_set, 1)

            def bias_block(e, blk):
                t0, t1 = BLOCKS[blk]
                dve.wait_ge(b2_in, (e + 1) * 16)
                for i in range(t1 - t0):
                    if t0 + i < t1 - 1:
                        dve.wait_ge(y_made, e * (CT - NB) + t0 - blk + i + 1)
                    else:
                        dve.wait_ge(stepped, e * STEPS + (blk + 1) * NF)
                    since(dve, added[i], uses(i, e, blk) * 16)
                    nc.vector.tensor_tensor(y_sb[:, i], y_ps[:, i], b2[:], ALU.add).then_inc(y_set, 1)

            for t in range(4):
                x_low(0, t)
            for f in range(AHEAD):
                w_low(0, f)
            for t in range(4, EARLY):
                x_low(0, t)

            def emit(e, first, last):
                for g in range(STEPS):
                    blk, f = divmod(g, NF)
                    n = (BLOCKS[blk][1] - BLOCKS[blk][0]) * P
                    dve.wait_ge(h_set, e * STEPS + g + 1)
                    nc.vector.tensor_tensor(h_lo[:, g % 2, 0:n], h[:, g % 2, 0:n], h_hi[:, g % 2, 0:n].bitcast(F32),
                                            ALU.subtract).then_inc(h_lo_set, 1)
                    if of := turn_at(g, e, last):
                        x_low(*of)
                    if of := refills_at(g, e, first, last):
                        w_low(*of)
                    if f == 0 and (g > 0 or not first):
                        bias_block(*((e, blk - 1) if blk else (e - 1, NB - 1)))

            experts(emit, dve)
            bias_block(E - 1, NB - 1)

        @block.tensor
        def _(pe):
            pe.wait_ge(ident_set, 2)
            pe.wait_ge(b1_in, 16)
            nc.tensor.transpose(t_ps[:, 1, 0:P], b1_rows[:], ident[:]).then_inc(b1_turned, 1)
            pe.wait_ge(b1_set, 1)

            def turn(e, t):
                pe.wait_ge(gathered[t % 2], (e * (CT // 2) + t // 2 + 1) * 16)
                since(pe, xT_lo_set, e * CT + t - 1)
                for c in range(ND):
                    last = nc.tensor.transpose(t_ps[:, t % 2, c * P:(c + 1) * P], x_rows[:, t % 2, c * P:(c + 1) * P],
                                               ident[:])
                last.then_inc(x_turned, 1)

            def first_product(e, g):
                blk, f = divmod(g, NF)
                t0, t1 = BLOCKS[blk]
                if blk == 0:
                    pe.wait_ge(w_lo_set, e * NF + f + 1)
                if f == 0:
                    pe.wait_ge(xT_lo_set, e * CT + t1)
                since(pe, h_set, e * STEPS + g - 1)
                for c in range(ND):
                    w = slice(c * P, (c + 1) * P)
                    last = product(nc, h_ps[:, g % 2, 0:(t1 - t0) * P], w_hi[:, f, w], w_lo[:, f, w],
                                   xT_hi[:, t0:t1, c], xT_lo[:, t0:t1, c], c == 0, c == ND - 1)
                last.then_inc(h_made, 1)

            def second_product(e, g):
                blk, f = divmod(g, NF)
                t0, t1 = BLOCKS[blk]
                pe.wait_ge(h_lo_set, e * STEPS + g + 1)
                for i in range(t1 - t0):
                    if f == 0:
                        b0, b1 = BLOCKS[blk - 1]
                        since(pe, y_set, (e if blk else e - 1) * CT + min(b0 + i + 1, b1))
                    t = slice(i * P, (i + 1) * P)
                    last = product(nc, y_ps[:, i], h_hi[:, g % 2, t], h_lo[:, g % 2, t],
                                   w_hi[:, f, D:2 * D], w_lo[:, f, D:2 * D], f == 0, f == NF - 1)
                    if f == NF - 1 and i < t1 - t0 - 1:
                        last.then_inc(y_made, 1)
                last.then_inc(stepped, 1)

            for t in range(EARLY):
                turn(0, t)

            def emit(e, first, last):
                for g in range(STEPS):
                    first_product(e, g)
                    if of := turn_at(g, e, last):
                        turn(*of)
                    if g > 0:
                        second_product(e, g - 1)
                    elif not first:
                        second_product(e - 1, STEPS - 1)

            experts(emit, pe)
            second_product(E - 1, STEPS - 1)


TABLE_KIND = "Internal"


def build(nc, a):
    attention_phase(nc, a)
    expert_phase(nc, a)


_INS = {"x": "x", "ctx": "ctx_1024", "mask": "mask_SxS2_bk0", "g_xattn": "g_xattn", "g_ffn": "g_ffn",
        "wq": "L0_xattn_Wq", "wk": "L0_xattn_Wk", "wv": "L0_xattn_Wv", "wo": "L0_xattn_Wo",
        "gate_w": "L0_ffn_gate_w", "gate_b": "L0_ffn_gate_b", "w1": "L0_ffn_w1", "b1": "L0_ffn_b1",
        "w2": "L0_ffn_w2", "b2": "L0_ffn_b2"}


def kernel(**inputs):
    import concourse.bacc as bacc
    from concourse.bass_utils import run_bass_kernel_spmd

    nc = bacc.Bacc("TRN2", target_bir_lowering=False, num_devices=1)
    arrays, a = {}, {}
    for name, of in _INS.items():
        v = np.ascontiguousarray(inputs[of])
        arrays[f"in_{name}"] = v
        a[name] = nc.dram_tensor(f"in_{name}", v.shape, mybir.dt.from_np(v.dtype), kind="ExternalInput").ap()
    a["out"] = nc.dram_tensor("out_rows", [ROWS, D], F32, kind="ExternalOutput").ap()
    a["xn2_table"] = nc.dram_tensor("xn2_table", [ROWS, D], F32, kind=TABLE_KIND).ap()
    a["slot_table"] = nc.dram_tensor("slot_table", [E * CAP, 2], I32, kind=TABLE_KIND).ap()
    build(nc, a)
    r = run_bass_kernel_spmd(nc, [arrays], core_ids=[0])
    return r.results[0]["out_rows"][:TOKENS].reshape(BATCHES, S, D)
```

```python
from contextlib import ExitStack

import numpy as np

import concourse.bass as bass
from concourse import mybir

ALU = mybir.AluOpType
ACT = mybir.ActivationFunctionType
AX = mybir.AxisListType
F32 = mybir.dt.float32
F32R = mybir.dt.float32r
I32 = mybir.dt.int32
U32 = mybir.dt.uint32
U8 = mybir.dt.uint8

P = 128
BATCHES, S, D = 16, 512, 512
TOKENS = BATCHES * S
NT = S // P
ND = D // P
QH, KVH, HD = 16, 4, 32
G = QH // KVH
PARTS = P // HD
UNITS = NT * KVH
E, TOP_K, FF = 8, 2, 2048
NF = FF // P
CAP = int(1.25 * TOKENS / E)
CT = CAP // P
ROWS = TOKENS + CAP
EPS = 1e-5
SCALE = float(HD) ** -0.5
MASKED = -3.0e38
FAR = 65536.0


def since(eng, sem, count, passed=None):
    if isinstance(count, int):
        if count > 0:
            eng.wait_ge(sem, count)
    else:
        eng.wait_ge(sem, count)
        if passed is not None:
            eng.sem_inc(passed, 1)


def product(nc, out, w_hi, w_lo, x_hi, x_lo, start, stop):
    nc.tensor.matmul(out, w_lo, x_hi, start=start, stop=False)
    nc.tensor.matmul(out, w_hi, x_lo, start=False, stop=False)
    return nc.tensor.matmul(out, w_hi, x_hi, start=False, stop=stop)


def attention_phase(nc, a):
    with ExitStack() as ctx:
        def sb(name, shape, dt=F32):
            return ctx.enter_context(nc.sbuf_tensor(name, shape, dt))

        def ps(name, shape):
            return ctx.enter_context(nc.psum_tensor(name, shape, F32))

        def sem(name):
            return ctx.enter_context(nc.semaphore(name))

        ident = sb("ident", [P, P])
        upto = sb("upto", [P, P])
        ones = sb("ones", [P, P])
        zeros = sb("zeros", [P, D])
        minus_half = sb("minus_half", [P, NT])
        expert_no = sb("expert_no", [P, E])
        slot_base = sb("slot_base", [P, E])
        unused = sb("unused", [P, E * CT, 2], I32)
        mask_u8 = sb("mask_u8", [P, NT, S], U8)
        mask_bias = sb("mask_bias", [P, NT, S])
        wk_raw = sb("wk_raw", [P, ND, P])
        wv_raw = sb("wv_raw", [P, ND, P])
        wo_raw = sb("wo_raw", [P, D])
        w_split = {n: (sb(f"w{n}_hi", [P, ND, P], F32R), sb(f"w{n}_lo", [P, ND, P], F32R)) for n in "qk"}
        wv_parts = sb("wv_parts", [P, ND, 2, P], F32R)
        wq_sum = sb("wq_sum", [P, ND, P])
        wo_hi, wo_lo = sb("wo_hi", [P, D], F32R), sb("wo_lo", [P, D], F32R)
        gate_w = sb("gate_w", [P, ND, E])
        gate_b = sb("gate_b", [P, E])
        g_raw = sb("g_raw", [P, 2])
        g_tanh = sb("g_tanh", [P, 2])

        x_sb = sb("x_sb", [P, NT, D])
        ctx_sb = sb("ctx_sb", [P, NT, D])
        xn = sb("xn", [P, NT, D])
        xT = (sb("xT_hi", [P, ND, S], F32R), sb("xT_lo", [P, ND, S], F32R))
        cT = (sb("cT_hi", [P, ND, S], F32R), sb("cT_lo", [P, ND, S], F32R))
        k_flat = (sb("k_hi", [P, S], F32R), sb("k_lo", [P, S], F32R))
        q_flat = (sb("q_hi", [P, S], F32R), sb("q_lo", [P, S], F32R))
        k_stack = [sb(f"k_stack{i}", [P, KVH, S], F32R) for i in range(2)]
        q_stack = [sb(f"q_stack{i}", [P, KVH, S], F32R) for i in range(2)]
        v_sb = [sb(f"v{i}", [P, NT, P]) for i in range(2)]
        stats = sb("stats", [P, NT, 6])
        mean_var = sb("mean_var", [P, NT, 2])
        rstd = sb("rstd", [P, NT])
        shift = sb("shift", [P, NT])
        probs = sb("probs", [P, 4, S])
        row_min = sb("row_min", [P, 4, 1])
        row_sum = sb("row_sum", [P, UNITS])
        pT_sb = sb("pT_sb", [P, 2, S])
        inv_sum = sb("inv_sum", [P, KVH])
        o_sb = sb("o_sb", [P, P])
        oT_hi, oT_lo = sb("oT_hi", [P, P], F32R), sb("oT_lo", [P, P], F32R)
        x_again = sb("x_again", [P, 2, D])
        x2 = sb("x2", [P, 2, D])
        stats2 = sb("stats2", [P, 6])
        mean_var2 = sb("mean_var2", [P, 2])
        rstd2 = sb("rstd2", [P, 1])
        shift2 = sb("shift2", [P, 1])
        xn2 = sb("xn2", [P, 2, D])
        xn2T = sb("xn2T", [P, ND, P])
        logits = sb("logits", [P, NT, E])
        best = sb("best", [P, NT, 8])
        best_no = sb("best_no", [P, NT, 8], U32)
        best_f = sb("best_f", [P, NT, TOP_K])
        chosen = sb("chosen", [P, TOP_K, NT, E])
        either = sb("either", [P, NT, E])
        before = sb("before", [P, E])
        prior = sb("prior", [P, NT, E])
        gap = sb("gap", [P, NT])
        ratio = sb("ratio", [P, NT])
        denom = sb("denom", [P, NT])
        share = sb("share", [P, NT])
        slot_e = sb("slot_e", [P, NT, E])
        over_e = sb("over_e", [P, NT, E])
        picked = sb("picked", [P, TOP_K, NT, E])
        slot_f = sb("slot_f", [P, TOP_K, NT])
        slot_i = sb("slot_i", [P, TOP_K, NT], I32)
        token_f = sb("token_f", [P, NT])
        info = sb("info", [P, TOP_K, NT, 2], I32)

        score_ps = ps("score_ps", [P, 2, S])
        pT_ps = ps("pT_ps", [P, 2, S])
        a_ps = ps("a_ps", [P, 2, S])
        y_ps = ps("y_ps", [P, S])
        o_bank = ps("o_bank", [P, S])
        o_ps, oT_ps, logit_ps = o_bank[:, 0:P], y_ps[:, 0:P], y_ps[:, 0:E]

        passed = sem("passed")
        wk_in = sem("wk_in")
        wv_in = sem("wv_in")
        wq_in = sem("wq_in")
        rest_in = sem("rest_in")
        consts_set = sem("consts_set")
        tanh_set = sem("tanh_set")
        prepared = sem("prepared")
        prep_step = sem("prep_step")
        padded = sem("padded")
        x_in = sem("x_in")
        ctx_in = sem("ctx_in")
        k_out = sem("k_out")
        q_out = sem("q_out")
        k_stacked = sem("k_stacked")
        q_stacked = sem("q_stacked")
        again_in = [sem(f"again_in{i}") for i in range(2)]
        x2_out = [sem(f"x2_out{i}") for i in range(2)]
        xn2_out = [sem(f"xn2_out{i}") for i in range(2)]
        routed = sem("routed")
        stats_set = sem("stats_set")
        aggr_set = sem("aggr_set")
        ln_step = sem("ln_step")
        xn_set = sem("xn_set")
        a_made = sem("a_made")
        a_hi = sem("a_hi")
        a_lo = sem("a_lo")
        scored = sem("scored")
        masked = sem("masked")
        exped = sem("exped")
        turned = sem("turned")
        pT_even = sem("pT_even")
        pT_odd = sem("pT_odd")
        weighed = sem("weighed")
        inv_set = sem("inv_set")
        o_set = sem("o_set")
        oT_made = sem("oT_made")
        oT_hi_set = sem("oT_hi_set")
        oT_lo_set = sem("oT_lo_set")
        y_made = sem("y_made")
        x2_set = sem("x2_set")
        stats2_set = sem("stats2_set")
        aggr2_set = sem("aggr2_set")
        ln2_step = sem("ln2_step")
        xn2_set = sem("xn2_set")
        xn2T_made = sem("xn2T_made")
        xn2T_set = sem("xn2T_set")
        logits_made = sem("logits_made")
        logits_set = sem("logits_set")
        gate_step = sem("gate_step")
        gate_pool = sem("gate_pool")
        ratio_set = sem("ratio_set")
        ranked = sem("ranked")
        before_step = sem("before_step")
        info_step = sem("info_step")

        A_STEPS = [("c", 0), ("c", 1), ("c", 2), ("c", 3), ("k", 0),
                   ("x", 0), ("x", 1), ("x", 2), ("x", 3), ("v", 0), ("q", 0), ("v", 1)]
        NA = len(A_STEPS)
        J_K, J_V, J_Q, J_X = (max(j for j, (what, _) in enumerate(A_STEPS) if what == w) for w in "kvqx")
        LOADS = 6
        S_X = 5
        NCONST = 13
        PREPARE_AT = {2: "k", J_K: "q", J_X + 1: "v", NA: "rest"}
        GD, GP = 11, 5
        RING = [("A", 0), ("A", 1), ("A", 2), ("X", 1), ("A", 3), ("A", 4), ("A", 5), ("A", 6), ("X", 2),
                ("A", 7), ("A", 8), ("A", 9), ("A", 10), ("X", 3), ("A", 11), ("X", 0), ("R", 0)]
        assert sum(what == "A" for what, _ in RING) == NA

        def ring_bank(user, par):
            return a_ps[:, (RING.index(user) + par * len(RING)) % 2]

        def ring_free(eng, user, b, through=0):
            r = RING.index(user)
            while True:
                r -= 2
                what, k = RING[r % len(RING)]
                of = b + r // len(RING)
                if isinstance(of, int) and of < -1:
                    return
                seq = {"A": of + 1, "X": of if k == 0 else of - 1, "R": of - 1}[what]
                if not isinstance(seq, int) or 0 <= seq < BATCHES:
                    break
            if through and not (what == "A" and r >= 0):
                since(eng, a_lo, (b + 1) * NA + through)
            if what == "A":
                since(eng, a_lo, seq * NA + (max(k + 1, through) if r >= 0 else k + 1))
            elif what == "X":
                since(eng, xn2T_set, seq * NT + k + 1)
            else:
                since(eng, gate_step, (seq + 1) * GD + 7)

        k_parked, q_parked = (nc.dram_tensor(n, [2, P, S], F32, kind="Internal").ap() for n in ("k_parts", "q_parts"))

        x_v = a["x"].rearrange("b (t p) d -> b p t d", p=P)
        c_v = a["ctx"].rearrange("b (t p) d -> b p t d", p=P)
        x_t = a["x"].rearrange("b (t p) d -> (b t) p d", p=P)
        out_t = a["out"].rearrange("(n p) d -> n p d", p=P)
        tab_t = a["xn2_table"].rearrange("(n p) d -> n p d", p=P)

        def bodies(emit, eng):
            emit(-1, 1, False, False, True)
            emit(0, 0, True, False, True)
            with eng.Fori(0, (BATCHES - 4) // 2) as i:
                emit(i * 2 + 1, 1, True, True, True)
                emit(i * 2 + 2, 0, True, True, True)
            emit(BATCHES - 3, 1, True, True, True)
            emit(BATCHES - 2, 0, True, True, True)
            emit(BATCHES - 1, 1, True, True, False)
            emit(BATCHES, 0, False, True, False)

        def due(slot, b, par, main, prev, n, first, every=1):
            for at, bb, pp, live in ((slot, b, par, main), (slot + UNITS, b - 1, 1 - par, prev)):
                k, rest = divmod(at - first, every)
                if live and rest == 0 and 0 <= k < n:
                    return k, bb, pp
            return None

        def normalises(b, slot, slots=1):
            at = slot - (9 if isinstance(b, int) and b < 0 else S_X)
            live = not isinstance(b, int) or b + 2 < BATCHES
            return [(b + 2, at)] if live and 0 <= at < slots else []

        block = ctx.enter_context(nc.Block())

        @block.sync
        def _(sp):
            sp.dma_start(ctx_sb[:], c_v[0]).then_inc(ctx_in, 16)
            sp.dma_start(wk_raw[:], a["wk"].rearrange("(c p) h e -> p c (h e)", p=P)).then_inc(wk_in, 16)
            sp.dma_start(x_sb[:], x_v[0]).then_inc(x_in, 16)
            sp.dma_start(mask_bias[:], a["wq"].rearrange("(c p) h e -> p c (h e)", p=P)).then_inc(wq_in, 16)
            sp.dma_start(wv_raw[:], a["wv"].rearrange("(c p) h e -> p c (h e)", p=P)).then_inc(wv_in, 16)
            loads = [(mask_u8[:], a["mask"].rearrange("(t p) k -> p t k", p=P)),
                     (wo_raw[:], a["wo"]),
                     (gate_w[:], a["gate_w"].rearrange("(c p) e -> p c e", p=P)),
                     (gate_b[:], a["gate_b"].partition_broadcast(P)),
                     (g_raw[:, 0:1], a["g_xattn"].partition_broadcast(P)),
                     (g_raw[:, 1:2], a["g_ffn"].partition_broadcast(P))]
            assert len(loads) == LOADS
            for to, of in loads:
                sp.dma_start(to, of).then_inc(rest_in, 16)
            sp.wait_ge(consts_set, NCONST)

            def emit(b, par, main, prev, nxt):
                n = b + 1
                for s in range(UNITS):
                    if isinstance(b, int) and b == 0 and s < (ROWS - TOKENS) // P:
                        sp.dma_start(out_t[TOKENS // P + s], zeros[:]).then_inc(padded, 16)
                        sp.dma_start(tab_t[TOKENS // P + s], zeros[:]).then_inc(padded, 16)
                    if s == 2 and nxt and not (isinstance(n, int) and n == BATCHES - 1):
                        since(sp, xn_set, n * NT + NT, passed)
                        sp.dma_start(x_sb[:], x_v[n + 1]).then_inc(x_in, 16)
                    if s == 5 and nxt and not (isinstance(n, int) and n == BATCHES - 1):
                        since(sp, a_made, n * NA + 4, passed)
                        sp.dma_start(ctx_sb[:], c_v[n + 1]).then_inc(ctx_in, 16)
                    if s == J_K + 1 and nxt:
                        park(n, k_parked, k_flat, J_K, k_out, k_stacked)
                    if s == J_K + 2 and nxt:
                        stack(n, k_stack[1 - par], k_parked, (0, 1, 0, 1), k_out, k_stacked)
                    if s == J_Q + 1 and nxt:
                        park(n, q_parked, q_flat, J_Q, q_out, q_stacked)
                    if s == J_Q + 2 and nxt:
                        stack(n, q_stack[1 - par], q_parked, (0, 0, 1, 1), q_out, q_stacked)
                    if it := due(s, b, par, main, prev, NT, 5, 4):
                        q, bb, _ = it
                        since(sp, x2_set, bb * NT + q - 1, passed)
                        sp.dma_start(x_again[:, q % 2], x_t[bb * NT + q]).then_inc(again_in[q % 2], 16)
                    if it := due(s, b, par, main, prev, NT, 11, 4):
                        q, bb, _ = it
                        since(sp, x2_set, bb * NT + q + 1, passed)
                        sp.dma_start(out_t[bb * NT + q], x2[:, q % 2]).then_inc(x2_out[q % 2], 16)
                    if it := due(s, b, par, main, prev, NT, 13, 4):
                        q, bb, _ = it
                        since(sp, xn2_set, bb * NT + q + 1, passed)
                        sp.dma_start(tab_t[bb * NT + q], xn2[:, q % 2]).then_inc(xn2_out[q % 2], 16)

            def park(n, to, of, j, out, stacked):
                since(sp, stacked, n * (PARTS * 16), passed)
                since(sp, a_hi, n * NA + j + 1, passed)
                since(sp, a_lo, n * NA + j + 1, passed)
                for part in range(2):
                    sp.dma_start(to[part], of[part][:].bitcast(F32)).then_inc(out, 16)

            def stack(n, to, of, parts, out, stacked):
                since(sp, out, (n + 1) * 32, passed)
                for g, part in enumerate(parts):
                    sp.dma_start(to[g * HD:(g + 1) * HD].bitcast(F32),
                                 of[part].rearrange("(h p) s -> p h s", p=HD)).then_inc(stacked, 16)

            bodies(emit, sp)
            sp.wait_ge(padded, 16 * 2 * ((ROWS - TOKENS) // P))
            for i in range(2):
                sp.wait_ge(x2_out[i], 16 * BATCHES * NT // 2)
                sp.wait_ge(xn2_out[i], 16 * BATCHES * NT // 2)

        @block.gpsimd
        def _(pool):
            nc.gpsimd.memset(ident[:], 0.0).then_inc(consts_set, 1)
            pool.wait_ge(consts_set, 1)
            nc.gpsimd.affine_select(out=ident[:], in_=ident[:], compare_op=ALU.not_equal, fill=1.0, base=0,
                                    pattern=[[-1, P]], channel_multiplier=1).then_inc(consts_set, 1)
            nc.gpsimd.memset(minus_half[:], -0.5).then_inc(consts_set, 1)
            nc.gpsimd.memset(unused[:], 0).then_inc(consts_set, 1)
            nc.gpsimd.memset(upto[:], 1.0).then_inc(consts_set, 1)
            nc.gpsimd.memset(zeros[:], 0.0).then_inc(consts_set, 1)
            nc.gpsimd.memset(ones[:], 1.0).then_inc(consts_set, 1)
            nc.gpsimd.memset(before[:], 0.0).then_inc(consts_set, 1)
            nc.gpsimd.iota(expert_no[:], [[1, E]], base=0, channel_multiplier=0,
                           allow_small_or_imprecise_dtypes=True).then_inc(consts_set, 1)
            nc.gpsimd.iota(slot_base[:], [[CAP, E]], base=-1, channel_multiplier=0,
                           allow_small_or_imprecise_dtypes=True).then_inc(consts_set, 1)
            nc.gpsimd.iota(token_f[:], [[P, NT]], base=0, channel_multiplier=1,
                           allow_small_or_imprecise_dtypes=True).then_inc(consts_set, 1)
            pool.wait_ge(consts_set, 11)
            nc.gpsimd.affine_select(out=upto[:], in_=upto[:], compare_op=ALU.is_ge, fill=0.0, base=0,
                                    pattern=[[1, P]], channel_multiplier=-1).then_inc(consts_set, 1)
            nc.gpsimd.iota(unused[:, :, 0].rearrange("p (e t) -> p e t", e=E), [[0, E], [P, CT]], base=TOKENS,
                           channel_multiplier=1).then_inc(consts_set, 1)
            pool.wait_ge(consts_set, NCONST)
            nc.gpsimd.dma_start(a["slot_table"].rearrange("(n p) c -> p n c", p=P), unused[:]).then_inc(routed, 16)

            def layernorm_scale(r, sh, mean, var, half, chain, done):
                nc.gpsimd.tensor_scalar(r, var, EPS, None, ALU.add).then_inc(chain, 1)
                nc.gpsimd.tensor_scalar(sh, mean, -1.0, None, ALU.mult).then_inc(chain, 1)
                since(pool, chain, done + 2, passed)
                nc.gpsimd.tensor_tensor(r, r, half, ALU.pow).then_inc(chain, 1)
                since(pool, chain, done + 3, passed)
                nc.gpsimd.tensor_tensor(sh, sh, r, ALU.mult).then_inc(chain, 1)
                since(pool, chain, done + 4, passed)

            def normalise(r):
                since(pool, aggr_set, r * NT + NT, passed)
                since(pool, xn_set, r * NT, passed)
                layernorm_scale(rstd[:], shift[:], mean_var[:, :, 0], mean_var[:, :, 1],
                                minus_half[:], ln_step, r * 4)
                since(pool, a_made, (r - 1) * NA + J_X + 1, passed)
                for t in range(NT):
                    nc.gpsimd.tensor_scalar(xn[:, t], x_sb[:, t], rstd[:, t:t + 1], shift[:, t:t + 1],
                                            ALU.mult, ALU.add).then_inc(xn_set, 1)

            def emit(b, par, main, prev, nxt):
                n = b + 1
                for s in range(UNITS):
                    if isinstance(b, int) and b < 0 and s == 1:
                        normalise(0)
                    for r, _ in normalises(b, s - NT):
                        normalise(r)
                    if it := due(s, b, par, main, prev, NT, 11, 4):
                        q, bb, _ = it
                        m = bb * NT + q
                        since(pool, aggr2_set, m + 1, passed)
                        since(pool, xn2_set, m, passed)
                        layernorm_scale(rstd2[:], shift2[:], mean_var2[:, 0:1], mean_var2[:, 1:2],
                                        minus_half[:, 0:1], ln2_step, m * 4)
                        since(pool, xn2_out[q % 2], (bb * 2 + q // 2) * 16, passed)
                        since(pool, xn2T_made, m - 1, passed)
                        nc.gpsimd.tensor_scalar(xn2[:, q % 2], x2[:, q % 2], rstd2[:], shift2[:],
                                                ALU.mult, ALU.add).then_inc(xn2_set, 1)
                    if it := due(s, b, par, main, prev, 1, 28):
                        _, bb, _ = it
                        since(pool, gate_step, (bb + 1) * GD + 4, passed)
                        nc.gpsimd.tensor_tensor(either[:], chosen[:, 0], chosen[:, 1], ALU.add).then_inc(gate_pool, 1)
                        nc.gpsimd.tensor_copy(prior[:, 0], before[:]).then_inc(gate_pool, 1)
                        nc.gpsimd.tensor_tensor(gap[:], best[:, :, 1], best[:, :, 0], ALU.subtract)\
                            .then_inc(gate_pool, 1)
                        since(pool, gate_pool, bb * GP + 3, passed)
                        for t in range(NT):
                            nc.gpsimd.tensor_tensor(prior[:, t + 1] if t < NT - 1 else before[:], prior[:, t],
                                                    either[:, t], ALU.add)\
                                .then_inc(before_step, 1)
                            since(pool, before_step, bb * NT + t + 1, passed)
                    if it := due(s, b, par, main, prev, 1, 30):
                        _, bb, _ = it
                        since(pool, gate_step, (bb + 1) * GD + 6, passed)
                        since(pool, routed, 16 + bb * (TOP_K * NT * 16), passed)
                        for k in range(TOP_K):
                            nc.gpsimd.tensor_copy(info[:, k, :, 0], token_f[:]).then_inc(info_step, 1)
                        nc.gpsimd.tensor_scalar(info[:, 0, :, 1].bitcast(F32), share[:], g_tanh[:, 1:2], None,
                                                ALU.mult).then_inc(info_step, 1)
                        nc.gpsimd.tensor_tensor(ratio[:], ratio[:], share[:], ALU.mult).then_inc(gate_pool, 1)
                        since(pool, gate_pool, bb * GP + 4, passed)
                        nc.gpsimd.tensor_scalar(info[:, 1, :, 1].bitcast(F32), ratio[:], g_tanh[:, 1:2], None,
                                                ALU.mult).then_inc(info_step, 1)
                        since(pool, info_step, bb * 4 + 4, passed)
                        nc.gpsimd.tensor_scalar(token_f[:], token_f[:], float(S), None, ALU.add).then_inc(gate_pool, 1)
                    if it := due(s, b, par, main, prev, 1, 31):
                        _, bb, _ = it
                        since(pool, gate_step, (bb + 1) * GD + GD, passed)
                        if isinstance(bb, int) and bb == 0:
                            pool.wait_ge(routed, 16)
                        for k in range(TOP_K):
                            for t in range(NT):
                                nc.gpsimd.indirect_dma_start(
                                    out=a["slot_table"], out_offset=bass.IndirectOffsetOnAxis(
                                        ap=slot_i[:, k, t:t + 1], axis=0),
                                    in_=info[:, k, t, :], in_offset=None,
                                    bounds_check=E * CAP - 1, oob_is_err=False).then_inc(routed, 16)

            bodies(emit, pool)
            pool.wait_ge(routed, 16 + BATCHES * (TOP_K * NT * 16))

        @block.scalar
        def _(act):
            def emit(b, par, main, prev, nxt):
                n = b + 1
                for s in range(UNITS):
                    if it := due(s, b, par, main, prev, UNITS, 1):
                        u, bb, _ = it
                        act.wait_ge(masked, bb * UNITS + u + 1)
                        nc.scalar.activation(probs[:, u % 4], probs[:, u % 4], ACT.Exp, bias=row_min[:, u % 4],
                                             scale=-1.0, accum_out=row_sum[:, u:u + 1]).then_inc(exped, 1)
                    if isinstance(b, int) and b < 0 and s == NA:
                        act.wait_ge(rest_in, 16 * LOADS)
                        nc.scalar.activation(g_tanh[:], g_raw[:], ACT.Tanh).then_inc(tanh_set, 1)
                    if nxt and s < NA:
                        what, k = A_STEPS[s]
                        bank = ring_bank(("A", s), par)
                        act.wait_ge(a_made, n * NA + s + 1)
                        if what in "cx":
                            since(act, a_made, (n - 1) * NA + (J_V if what == "c" else J_Q) + 1)
                            to = (cT if what == "c" else xT)[0][:, k]
                        elif what == "v":
                            to = v_sb[1 - par][:, 2 * k:2 * k + 2]
                            bank = bank.rearrange("p (t i e) -> p t i e", t=2, i=2)[:, :, 0]
                        else:
                            since(act, k_out if what == "k" else q_out, n * 32)
                            to = (k_flat if what == "k" else q_flat)[0][:]
                        nc.scalar.activation(to, bank, ACT.Copy).then_inc(a_hi, 1)
                    if it := due(s, b, par, main, prev, NT, 8, 4):
                        q, bb, _ = it
                        act.wait_ge(oT_made, bb * NT + q + 1)
                        since(act, y_made, bb * NT + q)
                        nc.scalar.activation(oT_hi[:], oT_ps, ACT.Copy).then_inc(oT_hi_set, 1)
                    if it := due(s, b, par, main, prev, NT, 14, 4):
                        q, bb, pp = it
                        act.wait_ge(xn2T_made, bb * NT + q + 1)
                        since(act, logits_made, bb * NT + q)
                        nc.scalar.activation(xn2T[:].rearrange("p c t -> p (c t)"), ring_bank(("X", q), par), ACT.Copy)\
                            .then_inc(xn2T_set, 1)
                    if (it := due(s, b, par, main, prev, UNITS, 2)) and it[0] % 2 == 0:
                        u, bb, _ = it
                        act.wait_ge(turned, bb * UNITS + u + 1)
                        since(act, weighed, bb * UNITS + u - 1)
                        nc.scalar.activation(pT_sb[:, 0], pT_ps[:, 0], ACT.Copy).then_inc(pT_even, 1)
                    if it := due(s, b, par, main, prev, 1, 29):
                        _, bb, _ = it
                        act.wait_ge(gate_pool, bb * GP + 3)
                        nc.scalar.activation(ratio[:], gap[:], ACT.Exp).then_inc(ratio_set, 1)

            bodies(emit, act)

        @block.vector
        def _(dve):
            prep = [0]

            def then(ins):
                prep[0] += 1
                ins.then_inc(prep_step, 1)
                dve.wait_ge(prep_step, prep[0])

            def split(*parts):
                for raw, hi, lo in parts:
                    last = nc.vector.tensor_copy(hi[:], raw[:])
                then(last)
                for raw, hi, lo in parts:
                    last = nc.vector.tensor_tensor(lo[:], raw[:], hi[:].bitcast(F32), ALU.subtract)
                return last

            def prepare(step):
                if step == "k":
                    dve.wait_ge(wk_in, 16)
                    split((wk_raw, *w_split["k"])).then_inc(prepared, 1)
                elif step == "v":
                    dve.wait_ge(wv_in, 16)
                    split((wv_raw, wv_parts[:, :, 0], wv_parts[:, :, 1])).then_inc(prepared, 1)
                elif step == "q":
                    dve.wait_ge(wq_in, 16)
                    for c in range(ND):
                        last = nc.vector.tensor_reduce(
                            wq_sum[:, c].rearrange("p (h e) -> p h e", h=KVH),
                            mask_bias[:, c].rearrange("p (h g e) -> p h e g", h=KVH, g=G), AX.X, ALU.add)
                    then(last)
                    split((wq_sum, *w_split["q"])).then_inc(prepared, 1)
                else:
                    dve.wait_ge(tanh_set, 1)
                    dve.wait_ge(rest_in, 16 * LOADS)
                    then(nc.vector.tensor_scalar(wo_raw[:], wo_raw[:], g_tanh[:, 0:1], None, ALU.mult))
                    split((wo_raw, wo_hi, wo_lo)).then_inc(gate_step, GD)
                    nc.vector.tensor_scalar(mask_bias[:], mask_u8[:], 1.0, -MASKED, ALU.subtract, ALU.mult)\
                        .then_inc(prepared, 1)
                    dve.wait_ge(prepared, 4)
                    dve.wait_ge(consts_set, NCONST)

            def x_stats(r, t):
                dve.wait_ge(x_in, (r + 1) * 16)
                nc.vector.bn_stats(stats[:, t], x_sb[:, t]).then_inc(stats_set, 1)

            def x_aggregate(r, t):
                since(dve, stats_set, r * NT + t + 1, passed)
                since(dve, ln_step, r * 4, passed)
                nc.vector.bn_aggr(mean_var[:, t], stats[:, t]).then_inc(aggr_set, 1)

            def emit(b, par, main, prev, nxt):
                n = b + 1
                for s in range(UNITS):
                    if it := due(s, b, par, main, prev, NT, 7, 4):
                        q, bb, _ = it
                        m = bb * NT + q
                        dve.wait_ge(weighed, bb * UNITS + 4 * q + 4)
                        dve.wait_ge(inv_set, m + 1)
                        since(dve, oT_made, m)
                        nc.vector.tensor_tensor(
                            o_sb[:].rearrange("p (h e) -> p h e", h=KVH),
                            o_ps.rearrange("p (h e) -> p h e", h=KVH),
                            inv_sum[:].unsqueeze(2).to_broadcast([P, KVH, HD]), ALU.mult).then_inc(o_set, 1)
                    if isinstance(b, int) and b < 0 and s in PREPARE_AT:
                        prepare(PREPARE_AT[s])
                    if main:
                        q, h = divmod(s, KVH)
                        since(dve, scored, b * UNITS + s + 1, passed)
                        since(dve, turned, b * UNITS + s - 3, passed)
                        nc.vector.tensor_tensor_reduce(probs[:, s % 4], score_ps[:, s % 2], mask_bias[:, q], -SCALE,
                                                       1e30, ALU.add, ALU.min, row_min[:, s % 4]).then_inc(masked, 1)
                    if nxt and s < NA:
                        what, k = A_STEPS[s]
                        bank = ring_bank(("A", s), par)
                        dve.wait_ge(a_hi, n * NA + s + 1)
                        if what == "v":
                            v = v_sb[1 - par][:, 2 * k:2 * k + 2]
                            nc.vector.tensor_tensor(v, bank.rearrange("p (t i e) -> p t i e", t=2, i=2)[:, :, 1], v,
                                                    ALU.add).then_inc(a_lo, 1)
                        else:
                            hi, lo = {"c": cT, "x": xT, "k": k_flat, "q": q_flat}[what]
                            if what in "cx":
                                hi, lo = hi[:, k], lo[:, k]
                            else:
                                hi, lo = hi[:], lo[:]
                            nc.vector.tensor_tensor(lo, bank, hi.bitcast(F32), ALU.subtract).then_inc(a_lo, 1)
                    if it := due(s, b, par, main, prev, NT, 8, 4):
                        q, bb, _ = it
                        dve.wait_ge(oT_hi_set, bb * NT + q + 1)
                        nc.vector.tensor_tensor(oT_lo[:], oT_ps, oT_hi[:].bitcast(F32), ALU.subtract)\
                            .then_inc(oT_lo_set, 1)
                    if it := due(s, b, par, main, prev, NT, 10, 4):
                        q, bb, _ = it
                        m = bb * NT + q
                        dve.wait_ge(y_made, m + 1)
                        dve.wait_ge(again_in[q % 2], (bb * 2 + q // 2 + 1) * 16)
                        since(dve, x2_out[q % 2], (bb * 2 + q // 2) * 16)
                        since(dve, xn2_set, m - 1)
                        nc.vector.tensor_tensor(x2[:, q % 2], y_ps[:], x_again[:, q % 2], ALU.add).then_inc(x2_set, 1)
                    if it := due(s, b, par, main, prev, NT, 11, 4):
                        q, bb, _ = it
                        dve.wait_ge(x2_set, bb * NT + q + 1)
                        nc.vector.bn_stats(stats2[:], x2[:, q % 2]).then_inc(stats2_set, 1)
                    if it := due(s, b, par, main, prev, NT, 6, 4):
                        q, bb, _ = it
                        dve.wait_ge(exped, bb * UNITS + 4 * q + 4)
                        since(dve, o_set, bb * NT + q)
                        nc.vector.reciprocal(inv_sum[:], row_sum[:, 4 * q:4 * q + 4]).then_inc(inv_set, 1)
                    if isinstance(b, int) and b < 0 and s == NT - 1:
                        for t in range(NT):
                            x_stats(0, t)
                        for t in range(NT):
                            x_aggregate(0, t)
                    for r, t in normalises(b, s - 1, NT):
                        x_aggregate(r, t)
                    if (it := due(s, b, par, main, prev, UNITS, 2)) and it[0] % 2 == 1:
                        u, bb, _ = it
                        dve.wait_ge(turned, bb * UNITS + u + 1)
                        since(dve, weighed, bb * UNITS + u - 1)
                        nc.vector.tensor_copy(pT_sb[:, 1], pT_ps[:, 1]).then_inc(pT_odd, 1)
                    if it := due(s, b, par, main, prev, NT, 11, 4):
                        q, bb, _ = it
                        m = bb * NT + q
                        since(dve, stats2_set, m + 1, passed)
                        since(dve, ln2_step, m * 4, passed)
                        nc.vector.bn_aggr(mean_var2[:], stats2[:]).then_inc(aggr2_set, 1)
                    if it := due(s, b, par, main, prev, NT, 15, 4):
                        q, bb, _ = it
                        dve.wait_ge(logits_made, bb * NT + q + 1)
                        nc.vector.tensor_tensor(logits[:, q], logit_ps, gate_b[:], ALU.add).then_inc(logits_set, 1)
                    for r, t in normalises(b, s, NT):
                        x_stats(r, t)
                    if it := due(s, b, par, main, prev, 1, 27):
                        _, bb, _ = it
                        g = (bb + 1) * GD
                        since(dve, logits_set, (bb + 1) * NT, passed)
                        for t in range(NT):
                            last = nc.vector.max(best[:, t], logits[:, t])
                        last.then_inc(gate_step, 1)
                        since(dve, gate_step, g + 1, passed)
                        for t in range(NT):
                            last = nc.vector.max_index(best_no[:, t], best[:, t], logits[:, t])
                        last.then_inc(gate_step, 1)
                        dve.wait_ge(gate_step, g + 2)
                        nc.vector.tensor_copy(best_f[:], best_no[:, :, 0:TOP_K]).then_inc(gate_step, 1)
                        dve.wait_ge(gate_step, g + 3)
                        for k in range(TOP_K):
                            last = nc.vector.tensor_tensor(
                                chosen[:, k], expert_no[:].unsqueeze(1).to_broadcast([P, NT, E]),
                                best_f[:, :, k:k + 1].to_broadcast([P, NT, E]), ALU.is_equal)
                        last.then_inc(gate_step, 1)
                    if it := due(s, b, par, main, prev, 1, 30):
                        _, bb, _ = it
                        g = (bb + 1) * GD
                        dve.wait_ge(ratio_set, bb + 1)
                        nc.vector.tensor_scalar(denom[:], ratio[:], 1.0, None, ALU.add).then_inc(gate_step, 1)
                        dve.wait_ge(gate_step, g + 5)
                        nc.vector.reciprocal(share[:], denom[:]).then_inc(gate_step, 1)
                    if it := due(s, b, par, main, prev, 1, 31):
                        _, bb, _ = it
                        g = (bb + 1) * GD
                        dve.wait_ge(ranked, bb + 1)
                        ranks = ring_bank(("R", 0), par)[:, 0:NT * E].rearrange("p (t e) -> p t e", e=E)
                        nc.vector.tensor_tensor(slot_e[:], ranks, slot_base[:].unsqueeze(1).to_broadcast([P, NT, E]),
                                                ALU.add)
                        nc.vector.tensor_scalar(over_e[:], ranks, float(CAP), FAR, ALU.is_gt, ALU.mult)\
                            .then_inc(gate_step, 1)
                        dve.wait_ge(gate_step, g + 7)
                        nc.vector.tensor_tensor(slot_e[:], slot_e[:], over_e[:], ALU.add).then_inc(gate_step, 1)
                        dve.wait_ge(gate_step, g + 8)
                        for k in range(TOP_K):
                            last = nc.vector.tensor_tensor(picked[:, k], chosen[:, k], slot_e[:], ALU.mult)
                        last.then_inc(gate_step, 1)
                        dve.wait_ge(gate_step, g + 9)
                        nc.vector.tensor_reduce(slot_f[:], picked[:], AX.X, ALU.add).then_inc(gate_step, 1)
                        dve.wait_ge(gate_step, g + 10)
                        since(dve, routed, 16 + bb * (TOP_K * NT * 16))
                        nc.vector.tensor_copy(slot_i[:], slot_f[:]).then_inc(gate_step, 1)

            bodies(emit, dve)

        @block.tensor
        def _(pe):
            pe.wait_ge(consts_set, 2)

            def turn(to, of):
                return nc.tensor.transpose(to, of, ident[:])

            def prepare(n, par, j):
                what, k = A_STEPS[j]
                bank = ring_bank(("A", j), 1 - par)
                through = {"k": J_K, "v": J_K, "q": J_X + 1}.get(what, 0)
                ring_free(pe, ("A", j), n - 1, through)
                if what in "cx":
                    if what == "c":
                        pe.wait_ge(ctx_in, (n + 1) * 16)
                    else:
                        pe.wait_ge(xn_set, (n + 1) * NT)
                    of = ctx_sb if what == "c" else xn
                    for t in range(NT):
                        last = turn(bank[:, t * P:(t + 1) * P], of[:, t, k * P:(k + 1) * P])
                else:
                    x_hi, x_lo = xT if what == "q" else cT
                    if what == "v":
                        for t in range(2):
                            tokens = slice((2 * k + t) * P, (2 * k + t + 1) * P)
                            both, hi = bank[:, t * 2 * P:(t + 1) * 2 * P], bank[:, t * 2 * P:(t * 2 + 1) * P]
                            for c in range(ND):
                                w = wv_parts[:, c].rearrange("p i e -> p (i e)")
                                if c == 0:
                                    nc.tensor.matmul(both, x_hi[:, c, tokens], w, start=True, stop=False)
                                nc.tensor.matmul(hi, x_lo[:, c, tokens], wv_parts[:, c, 0], start=False, stop=False)
                                if c > 0:
                                    last = nc.tensor.matmul(both, x_hi[:, c, tokens], w, start=False,
                                                            stop=(c == ND - 1))
                    else:
                        w_hi, w_lo = w_split[what]
                        for c in range(ND):
                            last = product(nc, bank, w_hi[:, c], w_lo[:, c], x_hi[:, c], x_lo[:, c],
                                           c == 0, c == ND - 1)
                last.then_inc(a_made, 1)

            def emit(b, par, main, prev, nxt):
                n = b + 1
                for s in range(UNITS):
                    if isinstance(b, int) and b < 0 and s < NA and A_STEPS[s][0] in "kqv":
                        pe.wait_ge(prepared, {"k": 1, "q": 2, "v": 3}[A_STEPS[s][0]])
                    if isinstance(b, int) and b == 0 and s == 0:
                        pe.wait_ge(prepared, 4)
                        pe.wait_ge(consts_set, NCONST)
                    if main:
                        q, h = divmod(s, KVH)
                        if s == 0:
                            pe.wait_ge(k_stacked, (b + 1) * (PARTS * 16))
                            pe.wait_ge(q_stacked, (b + 1) * (PARTS * 16))
                        since(pe, masked, b * UNITS + s - 1)
                        nc.tensor.matmul(score_ps[:, s % 2], q_stack[par][:, h, q * P:(q + 1) * P], k_stack[par][:, h],
                                         start=True, stop=True).then_inc(scored, 1)
                    if nxt and s < NA:
                        prepare(n, 1 - par, s)
                    if it := due(s, b, par, main, prev, UNITS, 2):
                        u, bb, _ = it
                        pe.wait_ge(exped, bb * UNITS + u + 1)
                        since(pe, pT_odd if u % 2 else pT_even, bb * (UNITS // 2) + u // 2)
                        for t in range(NT):
                            last = turn(pT_ps[:, u % 2, t * P:(t + 1) * P], probs[:, u % 4, t * P:(t + 1) * P])
                        last.then_inc(turned, 1)
                    if it := due(s, b, par, main, prev, NT, 8, 4):
                        q, bb, _ = it
                        m = bb * NT + q
                        pe.wait_ge(o_set, m + 1)
                        since(pe, x2_set, m)
                        since(pe, logits_set, m - 1)
                        turn(oT_ps, o_sb[:]).then_inc(oT_made, 1)
                    if it := due(s, b, par, main, prev, NT, 14, 4):
                        q, bb, pp = it
                        bank = ring_bank(("X", q), par)
                        pe.wait_ge(xn2_set, bb * NT + q + 1)
                        ring_free(pe, ("X", q), b)
                        for c in range(ND):
                            last = turn(bank[:, c * P:(c + 1) * P], xn2[:, q % 2, c * P:(c + 1) * P])
                        last.then_inc(xn2T_made, 1)
                    if it := due(s, b, par, main, prev, NT, 15, 4):
                        q, bb, _ = it
                        pe.wait_ge(xn2T_set, bb * NT + q + 1)
                        since(pe, logits_set, bb * NT + q)
                        y_count = bb * NT + q + 2
                        pe.wait_ge(x2_set, min(y_count, BATCHES * NT) if isinstance(y_count, int) else y_count)
                        for c in range(ND):
                            last = nc.tensor.matmul(logit_ps, xn2T[:, c], gate_w[:, c],
                                                    start=(c == 0), stop=(c == ND - 1))
                        last.then_inc(logits_made, 1)
                    if it := due(s, b, par, main, prev, 1, 31):
                        _, bb, _ = it
                        pe.wait_ge(before_step, bb * NT + NT)
                        ring_free(pe, ("R", 0), b)
                        to = ring_bank(("R", 0), par)[:, 0:NT * E]
                        nc.tensor.matmul(to, upto[:], either[:].rearrange("p t e -> p (t e)"), start=True, stop=False)
                        nc.tensor.matmul(to, ones[:], prior[:].rearrange("p t e -> p (t e)"), start=False, stop=True)\
                            .then_inc(ranked, 1)
                    if it := due(s, b, par, main, prev, UNITS, 3):
                        u, bb, pp = it
                        q, h = divmod(u, KVH)
                        pe.wait_ge(pT_odd if u % 2 else pT_even, bb * (UNITS // 2) + u // 2 + 1)
                        if u == 0:
                            pe.wait_ge(a_lo, bb * NA + J_V + 1)
                        if h == 0:
                            since(pe, o_set, bb * NT + q)
                        for t in range(NT):
                            last = nc.tensor.matmul(o_ps[:, h * HD:(h + 1) * HD], pT_sb[:, u % 2, t * P:(t + 1) * P],
                                                    v_sb[pp][:, t, h * HD:(h + 1) * HD],
                                                    start=(t == 0), stop=(t == NT - 1))
                        last.then_inc(weighed, 1)
                    if it := due(s, b, par, main, prev, NT, 9, 4):
                        q, bb, _ = it
                        m = bb * NT + q
                        pe.wait_ge(oT_hi_set, m + 1)
                        pe.wait_ge(oT_lo_set, m + 1)
                        product(nc, y_ps[:], oT_hi[:], oT_lo[:], wo_hi[:], wo_lo[:], True, True).then_inc(y_made, 1)

            bodies(emit, pe)


def expert_phase(nc, a):
    with ExitStack() as ctx:
        def sb(name, shape, dt=F32):
            return ctx.enter_context(nc.sbuf_tensor(name, shape, dt))

        def ps(name, shape):
            return ctx.enter_context(nc.psum_tensor(name, shape, F32))

        def sem(name):
            return ctx.enter_context(nc.semaphore(name))

        BLOCKS = [(0, 4), (4, 7), (7, 10)]
        NB = len(BLOCKS)
        STEPS = NB * NF
        WIDE = max(t1 - t0 for t0, t1 in BLOCKS)
        EARLY = BLOCKS[0][1]

        ident = sb("ident2", [P, P])
        w_hi = sb("w_hi", [P, NF, 2 * D], F32R)
        w_lo = sb("w_lo", [P, NF, 2 * D], F32R)
        staged = sb("staged", [P, 2, 2 * D])
        x_rows = sb("x_rows", [P, 2, D])
        xT_hi = sb("xT2_hi", [P, CT, ND, P], F32R)
        xT_lo = sb("xT2_lo", [P, CT, ND, P], F32R)
        h = sb("h", [P, 2, WIDE * P])
        h_hi = sb("h_hi", [P, 2, WIDE * P], F32R)
        h_lo = sb("h_lo", [P, 2, WIDE * P], F32R)
        y_sb = sb("y_sb", [P, WIDE, D])
        b1_rows = sb("b1_rows", [P, P])
        b1T = sb("b1T", [P, E * NF])
        b2 = sb("b2", [P, D])
        take = sb("take", [P, CT, 2], I32)
        give = sb("give", [P, CT, 2], I32)

        h_ps = ps("h_ps", [P, 2, D])
        y_ps = ps("y2_ps", [P, WIDE, D])
        t_ps = ps("t_ps", [P, 2, D])

        passed = sem("passed2")
        ident_set = sem("ident2_set")
        b1_in = sem("b1_in")
        b1_turned = sem("b1_turned")
        b1_set = sem("b1_set")
        b2_in = sem("b2_in")
        take_in = sem("take_in")
        give_in = sem("give_in")
        staged_in = [sem(f"staged_in{i}") for i in range(2)]
        w_hi_set = sem("w_hi_set")
        w_lo_set = sem("w_lo_set")
        gathered = [sem(f"gathered{i}") for i in range(2)]
        first_in = [sem(f"first_in{i}") for i in range(EARLY)]
        x_turned = sem("x_turned")
        xT_hi_set = sem("xT2_hi_set")
        xT_lo_set = sem("xT2_lo_set")
        h_made = sem("h_made")
        h_set = sem("h_set")
        h_lo_set = sem("h_lo_set")
        stepped = sem("stepped")
        y_made = sem("y2_made")
        y_set = sem("y_set")
        y_weighed = sem("y_weighed")
        added = [sem(f"added{i}") for i in range(WIDE)]

        w1_v = a["w1"].rearrange("e (c p) (f m) -> e f p c m", p=P, m=P)
        w2_v = a["w2"].rearrange("e (f p) d -> e f p d", p=P)
        slots_v = a["slot_table"].rearrange("(e t p) c -> e p t c", p=P, t=CT)

        def block_of(t):
            return next(i for i, (t0, t1) in enumerate(BLOCKS) if t0 <= t < t1)

        TURNS = {4: (0, 7), 7: (0, 8), 10: (0, 9), 19: (1, 0), 22: (1, 1), 25: (1, 2), 28: (1, 3),
                 35: (1, 4), 38: (1, 5), 41: (1, 6)}
        AHEAD = 3

        def turn_at(g, e, first, last):
            if first and 1 <= g < 4:
                return e, EARLY + g - 1
            if g in TURNS:
                later, t = TURNS[g]
                if not (later and last):
                    return e + later, t
            return None

        def refills_at(g, e, first, last):
            if first and g + AHEAD < NF:
                return e, g + AHEAD
            if not first and g < 2:
                return e, NF - 2 + g
            if not last and g >= STEPS - NF + 2:
                return e + 1, g - (STEPS - NF + 2)
            return None

        def experts(emit, eng):
            emit(0, True, False)
            with eng.Fori(1, E - 1) as e:
                emit(e, False, False)
            emit(E - 1, False, True)

        def gathers_to(e, t):
            return e * (CT // 2) + t // 2 + 1 - EARLY // 2

        def uses(i, e, blk):
            return e * sum(i < t1 - t0 for t0, t1 in BLOCKS) + sum(i < t1 - t0 for t0, t1 in BLOCKS[:blk])

        block = ctx.enter_context(nc.Block())

        @block.sync
        def _(sp):
            def stage(e, f):
                since(sp, w_lo_set, e * NF + f - 1, passed)
                sp.dma_start(staged[:, f % 2, 0:D].rearrange("p (c m) -> p c m", c=ND), w1_v[e, f])\
                    .then_inc(staged_in[f % 2], 16)
                sp.dma_start(staged[:, f % 2, D:2 * D], w2_v[e, f]).then_inc(staged_in[f % 2], 16)

            sp.dma_start(take[:], slots_v[0]).then_inc(take_in, 16)
            stage(0, 0)
            stage(0, 1)
            sp.dma_start(b1_rows[:], a["b1"].rearrange("e (f m) -> (e f) m", m=P)).then_inc(b1_in, 16)
            stage(0, 2)

            def emit(e, first, last):
                for g in range(STEPS):
                    if g == 3:
                        for i in range(WIDE):
                            since(sp, added[i], uses(i, e, 0) * 16, passed)
                        sp.dma_start(give[:], slots_v[e]).then_inc(give_in, 16)
                        since(sp, y_set, e * CT, passed)
                        sp.dma_start(b2[:], a["b2"][e].partition_broadcast(P)).then_inc(b2_in, 16)
                    if g == 6 and not last:
                        for i in range(2):
                            since(sp, gathered[i], gathers_to(e, CT - 2 + i) * 16, passed)
                        sp.dma_start(take[:], slots_v[e + 1]).then_inc(take_in, 16)
                    if of := refills_at(g, e, first, last):
                        stage(*of)

            experts(emit, sp)
            for i in range(WIDE):
                sp.wait_ge(added[i], uses(i, E, 0) * 16)

        @block.gpsimd
        def _(pool):
            nc.gpsimd.memset(ident[:], 0.0).then_inc(ident_set, 1)
            pool.wait_ge(ident_set, 1)
            nc.gpsimd.affine_select(out=ident[:], in_=ident[:], compare_op=ALU.not_equal, fill=1.0, base=0,
                                    pattern=[[-1, P]], channel_multiplier=1).then_inc(ident_set, 1)

            def gather(e, t):
                since(pool, take_in, (e + 1) * 16, passed)
                since(pool, x_turned, e * CT + t - 1, passed)
                nc.gpsimd.indirect_dma_start(
                    out=x_rows[:, t % 2], out_offset=None, in_=a["xn2_table"],
                    in_offset=bass.IndirectOffsetOnAxis(ap=take[:, t, 0:1], axis=0)).then_inc(gathered[t % 2], 16)

            pool.wait_ge(take_in, 16)
            for t in range(EARLY):
                nc.gpsimd.indirect_dma_start(
                    out=y_sb[:, t], out_offset=None, in_=a["xn2_table"],
                    in_offset=bass.IndirectOffsetOnAxis(ap=take[:, t, 0:1], axis=0)).then_inc(first_in[t], 16)
            for t in range(EARLY, EARLY + 2):
                gather(0, t)

            def emit(e, first, last):
                for g in range(STEPS):
                    if of := turn_at(g, e, first, last):
                        ee, t = of
                        if t + 2 < CT:
                            gather(ee, t + 2)
                        elif not last:
                            gather(ee + 1, t + 2 - CT)
                    if g % NF == 2 and (g > 2 or not first):
                        scatter_block(*((e, g // NF - 1) if g > 2 else (e - 1, NB - 1)))

            def scatter_block(e, blk):
                t0, t1 = BLOCKS[blk]
                since(pool, give_in, (e + 1) * 16, passed)
                if blk == 0:
                    for i in range(WIDE):
                        since(pool, added[i], uses(i, e, 0) * 16, passed)
                for i in range(t1 - t0):
                    since(pool, y_weighed, e * CT + t0 + i + 1, passed)
                    nc.gpsimd.indirect_dma_start(
                        out=a["out"], out_offset=bass.IndirectOffsetOnAxis(ap=give[:, t0 + i, 0:1], axis=0),
                        in_=y_sb[:, i], in_offset=None, compute_op=ALU.add).then_inc(added[i], 16)

            experts(emit, pool)
            scatter_block(E - 1, NB - 1)

        @block.scalar
        def _(act):
            act.wait_ge(b1_turned, 1)
            nc.scalar.activation(b1T[:], t_ps[:, 1, 0:P], ACT.Copy).then_inc(b1_set, 1)

            def x_high(e, t):
                act.wait_ge(x_turned, e * CT + t + 1)
                since(act, h_made, (e - 1) * STEPS + NF * (block_of(t) + 1))
                nc.scalar.activation(xT_hi[:, t].rearrange("p c t -> p (c t)"), t_ps[:, t % 2], ACT.Copy)\
                    .then_inc(xT_hi_set, 1)

            def w_high(e, f):
                act.wait_ge(staged_in[f % 2], (e * (NF // 2) + f // 2 + 1) * 32)
                since(act, stepped, (e - 1) * STEPS + (NB - 1) * NF + f + 1)
                nc.scalar.activation(w_hi[:, f], staged[:, f % 2], ACT.Copy).then_inc(w_hi_set, 1)

            def weigh_block(e, blk):
                t0, t1 = BLOCKS[blk]
                act.wait_ge(give_in, (e + 1) * 16)
                for i in range(t1 - t0):
                    act.wait_ge(y_set, e * CT + t0 + i + 1)
                    nc.scalar.activation(y_sb[:, i], y_sb[:, i], ACT.Copy,
                                         scale=give[:, t0 + i, 1:2].bitcast(F32)).then_inc(y_weighed, 1)

            w_high(0, 0)
            for t in range(EARLY):
                x_high(0, t)
            for f in range(1, AHEAD):
                w_high(0, f)

            def emit(e, first, last):
                for g in range(STEPS):
                    blk, f = divmod(g, NF)
                    n = (BLOCKS[blk][1] - BLOCKS[blk][0]) * P
                    since(act, h_made, e * STEPS + g + 1, passed)
                    since(act, stepped, e * STEPS + g - 1, passed)
                    bias = b1T[:, bass.ds(e * NF + f, 1)]
                    nc.scalar.activation(h[:, g % 2, 0:n], h_ps[:, g % 2, 0:n], ACT.Relu, bias=bias)
                    nc.scalar.activation(h_hi[:, g % 2, 0:n], h_ps[:, g % 2, 0:n], ACT.Relu, bias=bias)\
                        .then_inc(h_set, 1)
                    if of := turn_at(g, e, first, last):
                        x_high(*of)
                    if of := refills_at(g, e, first, last):
                        w_high(*of)
                    if f == 1 and (g > 1 or not first):
                        weigh_block(*((e, blk - 1) if blk else (e - 1, NB - 1)))

            experts(emit, act)
            weigh_block(E - 1, NB - 1)

        @block.vector
        def _(dve):
            def x_low(e, t):
                dve.wait_ge(xT_hi_set, e * CT + t + 1)
                nc.vector.tensor_tensor(xT_lo[:, t].rearrange("p c t -> p (c t)"), t_ps[:, t % 2],
                                        xT_hi[:, t].rearrange("p c t -> p (c t)").bitcast(F32), ALU.subtract)\
                    .then_inc(xT_lo_set, 1)

            def w_low(e, f):
                dve.wait_ge(w_hi_set, e * NF + f + 1)
                nc.vector.tensor_tensor(w_lo[:, f], staged[:, f % 2], w_hi[:, f].bitcast(F32), ALU.subtract)\
                    .then_inc(w_lo_set, 1)

            def bias_block(e, blk):
                t0, t1 = BLOCKS[blk]
                dve.wait_ge(b2_in, (e + 1) * 16)
                for i in range(t1 - t0):
                    if t0 + i < t1 - 1:
                        dve.wait_ge(y_made, e * (CT - NB) + t0 - blk + i + 1)
                    else:
                        dve.wait_ge(stepped, e * STEPS + (blk + 1) * NF)
                    since(dve, added[i], uses(i, e, blk) * 16)
                    nc.vector.tensor_tensor(y_sb[:, i], y_ps[:, i], b2[:], ALU.add).then_inc(y_set, 1)

            w_low(0, 0)
            for t in range(EARLY):
                x_low(0, t)
            for f in range(1, AHEAD):
                w_low(0, f)

            def emit(e, first, last):
                for g in range(STEPS):
                    blk, f = divmod(g, NF)
                    n = (BLOCKS[blk][1] - BLOCKS[blk][0]) * P
                    dve.wait_ge(h_set, e * STEPS + g + 1)
                    nc.vector.tensor_tensor(h_lo[:, g % 2, 0:n], h[:, g % 2, 0:n], h_hi[:, g % 2, 0:n].bitcast(F32),
                                            ALU.subtract).then_inc(h_lo_set, 1)
                    if of := turn_at(g, e, first, last):
                        x_low(*of)
                    if of := refills_at(g, e, first, last):
                        w_low(*of)
                    if f == 0 and (g > 0 or not first):
                        bias_block(*((e, blk - 1) if blk else (e - 1, NB - 1)))

            experts(emit, dve)
            bias_block(E - 1, NB - 1)

        @block.tensor
        def _(pe):
            pe.wait_ge(ident_set, 2)
            pe.wait_ge(b1_in, 16)
            nc.tensor.transpose(t_ps[:, 1, 0:P], b1_rows[:], ident[:]).then_inc(b1_turned, 1)
            pe.wait_ge(b1_set, 1)

            def turn(e, t, early=False):
                if early:
                    pe.wait_ge(first_in[t], 16)
                else:
                    pe.wait_ge(gathered[t % 2], gathers_to(e, t) * 16)
                since(pe, xT_lo_set, e * CT + t - 1)
                for c in range(ND):
                    last = nc.tensor.transpose(t_ps[:, t % 2, c * P:(c + 1) * P],
                                               (y_sb[:, t] if early else x_rows[:, t % 2])[:, c * P:(c + 1) * P],
                                               ident[:])
                last.then_inc(x_turned, 1)

            def first_product(e, g):
                blk, f = divmod(g, NF)
                t0, t1 = BLOCKS[blk]
                if blk == 0:
                    pe.wait_ge(w_lo_set, e * NF + f + 1)
                if f == 0:
                    pe.wait_ge(xT_lo_set, e * CT + t1)
                since(pe, h_set, e * STEPS + g - 1)
                for c in range(ND):
                    w = slice(c * P, (c + 1) * P)
                    last = product(nc, h_ps[:, g % 2, 0:(t1 - t0) * P], w_hi[:, f, w], w_lo[:, f, w],
                                   xT_hi[:, t0:t1, c], xT_lo[:, t0:t1, c], c == 0, c == ND - 1)
                last.then_inc(h_made, 1)

            def second_product(e, g):
                blk, f = divmod(g, NF)
                t0, t1 = BLOCKS[blk]
                pe.wait_ge(h_lo_set, e * STEPS + g + 1)
                for i in range(t1 - t0):
                    if f == 0:
                        b0, b1 = BLOCKS[blk - 1]
                        since(pe, y_set, (e if blk else e - 1) * CT + min(b0 + i + 1, b1))
                    t = slice(i * P, (i + 1) * P)
                    last = product(nc, y_ps[:, i], h_hi[:, g % 2, t], h_lo[:, g % 2, t],
                                   w_hi[:, f, D:2 * D], w_lo[:, f, D:2 * D], f == 0, f == NF - 1)
                    if f == NF - 1 and i < t1 - t0 - 1:
                        last.then_inc(y_made, 1)
                last.then_inc(stepped, 1)

            for t in range(EARLY):
                turn(0, t, early=True)

            def emit(e, first, last):
                for g in range(STEPS):
                    first_product(e, g)
                    if of := turn_at(g, e, first, last):
                        turn(*of)
                    if g > 0:
                        second_product(e, g - 1)
                    elif not first:
                        second_product(e - 1, STEPS - 1)

            experts(emit, pe)
            second_product(E - 1, STEPS - 1)


TABLE_KIND = "Internal"


def build(nc, a):
    attention_phase(nc, a)
    expert_phase(nc, a)


_INS = {"x": "x", "ctx": "ctx_1024", "mask": "mask_SxS2_bk0", "g_xattn": "g_xattn", "g_ffn": "g_ffn",
        "wq": "L0_xattn_Wq", "wk": "L0_xattn_Wk", "wv": "L0_xattn_Wv", "wo": "L0_xattn_Wo",
        "gate_w": "L0_ffn_gate_w", "gate_b": "L0_ffn_gate_b", "w1": "L0_ffn_w1", "b1": "L0_ffn_b1",
        "w2": "L0_ffn_w2", "b2": "L0_ffn_b2"}


def kernel(**inputs):
    import concourse.bacc as bacc
    from concourse.bass_utils import run_bass_kernel_spmd

    nc = bacc.Bacc("TRN2", target_bir_lowering=False, num_devices=1)
    arrays, a = {}, {}
    for name, of in _INS.items():
        v = np.ascontiguousarray(inputs[of])
        arrays[f"in_{name}"] = v
        a[name] = nc.dram_tensor(f"in_{name}", v.shape, mybir.dt.from_np(v.dtype), kind="ExternalInput").ap()
    a["out"] = nc.dram_tensor("out_rows", [ROWS, D], F32, kind="ExternalOutput").ap()
    a["xn2_table"] = nc.dram_tensor("xn2_table", [ROWS, D], F32, kind=TABLE_KIND).ap()
    a["slot_table"] = nc.dram_tensor("slot_table", [E * CAP, 2], I32, kind=TABLE_KIND).ap()
    build(nc, a)
    r = run_bass_kernel_spmd(nc, [arrays], core_ids=[0])
    return r.results[0]["out_rows"][:TOKENS].reshape(BATCHES, S, D)
```
